# Optimizing a Trainium2 kernel written in Bass

```python
import numpy as np
import jax
import jax.numpy as jnp

def _softmax(x, axis=-1):
    return jax.nn.softmax(x, axis=axis)

def _gelu(x):
    return jax.nn.gelu(x, approximate=True)

def _silu(x):
    return jax.nn.silu(x)

def _sigmoid(x):
    return jax.nn.sigmoid(x)

def _layernorm(x, axis=-1, eps=1e-05):
    m = jnp.mean(x, axis=axis, keepdims=True)
    v = jnp.var(x, axis=axis, keepdims=True)
    return (x - m) / jnp.sqrt(v + eps)

def _scatter_add(tgt, idx, src, axis=0):
    return tgt.at[idx].add(src)

def _segment_sum(src, seg, n):
    return jax.ops.segment_sum(src, seg, n)
kernel_name = 'mk_decoder_postln_d1_seqx_r4_c3125a'

def setup_inputs(seed: int=0):
    np.random.seed(seed)
    _w = jnp.asarray

    def _rec_inputs():
        import jax
        import jax.numpy as jnp
        _rk = jax.random.key(seed)
        x = -0.0002928 + 1 * jax.random.normal(jax.random.fold_in(_rk, 1), (128, 128, 256), jnp.float32)
        _lenS = 128 - jax.random.randint(jax.random.fold_in(_rk, 7), (128,), 0, max(1, 128 // 4) + 1, jnp.int32)
        _lenS2 = 128 - jax.random.randint(jax.random.fold_in(_rk, 8), (128,), 0, max(1, 128 // 4) + 1, jnp.int32)
        _ctx_1024P = jax.random.normal(jax.random.fold_in(_rk, 11), (128, 16, 256), jnp.float32)
        _ctx_1024c = jax.random.dirichlet(jax.random.fold_in(_rk, 511), 0.3 * jnp.ones((16,), jnp.float32), (128, 128))
        _ctx_1024t = jnp.einsum('bsk,bkd->bsd', _ctx_1024c, _ctx_1024P)
        _ctx_1024t = _ctx_1024t * jax.lax.rsqrt(jnp.mean(jnp.square(_ctx_1024t)) + 1e-12) * 0.953939
        ctx_1024 = -1.39393e-06 + 0.999914 * (_ctx_1024t + 0.3 * jax.random.normal(jax.random.fold_in(_rk, 611), (128, 128, 256), jnp.float32))
        return (x, ctx_1024)
    x, ctx_1024 = _rec_inputs()

    def _L0_attn_setup():
        import jax, jax.numpy as jnp
        import numpy as np
        NUM_HEADS = 16
        key = jax.random.key(seed)
        ks = jax.random.split(key, 5)
        B, S, H = (2, 512, 256)
        scale = 0.02
        return {'x': jax.random.normal(ks[0], (B, S, H), dtype=jnp.float32), 'w_qkv': jax.random.normal(ks[1], (H, 3 * H), dtype=jnp.float32) * scale, 'b_qkv': jax.random.normal(ks[2], (3 * H,), dtype=jnp.float32) * scale, 'w_out': jax.random.normal(ks[3], (H, H), dtype=jnp.float32) * scale, 'b_out': jax.random.normal(ks[4], (H,), dtype=jnp.float32) * scale}
    _L0_attn_all = _L0_attn_setup()
    _L0_attn_in = {k: v for k, v in _L0_attn_all.items() if k in ('w_qkv', 'b_qkv', 'w_out', 'b_out')}
    del _L0_attn_all

    def _L0_xattn_setup():
        import jax, jax.numpy as jnp
        import numpy as np
        B, T, N_EMBD, N_HEAD = (2, 512, 256, 16)
        HEAD = N_EMBD // N_HEAD
        WINDOW = 64
        key = jax.random.key(seed)
        kq, kk, kv, kw = jax.random.split(key, 4)
        q = jax.random.normal(kq, (B, T, N_EMBD), dtype=jnp.float32)
        k = jax.random.normal(kk, (B, T, N_EMBD), dtype=jnp.float32)
        v = jax.random.normal(kv, (B, T, N_EMBD), dtype=jnp.float32)
        W_proj = jax.random.normal(kw, (N_EMBD, N_EMBD), dtype=jnp.float32) * (1.0 / np.sqrt(N_EMBD))
        b_proj = jnp.zeros((N_EMBD,), dtype=jnp.float32)
        return {'q': q, 'k': k, 'v': v, 'W_proj': W_proj, 'b_proj': b_proj}
    _L0_xattn_all = _L0_xattn_setup()
    _L0_xattn_in = {k: v for k, v in _L0_xattn_all.items() if k in ('W_proj', 'b_proj')}
    del _L0_xattn_all

    def _L0_ffn_setup():
        import jax, jax.numpy as jnp
        import numpy as np
        B, N, D, E, R, K = (4, 512, 256, 8, 64, 2)
        key = jax.random.key(seed)
        ks = jax.random.split(key, 5)
        scale = 0.02
        return {'x': jax.random.normal(ks[0], (B, N, D), dtype=jnp.float32), 'gate_w': jax.random.normal(ks[1], (D, E), dtype=jnp.float32) * scale, 'Wu': jax.random.normal(ks[2], (E, D, R), dtype=jnp.float32) * scale, 'Wv': jax.random.normal(ks[3], (E, D, R), dtype=jnp.float32) * scale, 'Wo': jax.random.normal(ks[4], (E, R, D), dtype=jnp.float32) * scale}
    _L0_ffn_all = _L0_ffn_setup()
    _L0_ffn_in = {k: v for k, v in _L0_ffn_all.items() if k in ('gate_w', 'Wu', 'Wv', 'Wo')}
    del _L0_ffn_all
    return {'x': x, 'ctx_1024': ctx_1024, 'L0_attn_w_qkv': _L0_attn_in['w_qkv'], 'L0_attn_b_qkv': _L0_attn_in['b_qkv'], 'L0_attn_w_out': _L0_attn_in['w_out'], 'L0_attn_b_out': _L0_attn_in['b_out'], 'L0_xattn_W_proj': _L0_xattn_in['W_proj'], 'L0_xattn_b_proj': _L0_xattn_in['b_proj'], 'L0_ffn_gate_w': _L0_ffn_in['gate_w'], 'L0_ffn_Wu': _L0_ffn_in['Wu'], 'L0_ffn_Wv': _L0_ffn_in['Wv'], 'L0_ffn_Wo': _L0_ffn_in['Wo']}

def reference(x, ctx_1024, L0_attn_w_qkv, L0_attn_b_qkv, L0_attn_w_out, L0_attn_b_out, L0_xattn_W_proj, L0_xattn_b_proj, L0_ffn_gate_w, L0_ffn_Wu, L0_ffn_Wv, L0_ffn_Wo):
    import jax
    import jax.numpy as jnp

    def _L0_attn_ref(x, w_qkv, b_qkv, w_out, b_out):
        import jax, jax.numpy as jnp
        import numpy as np
        NUM_HEADS = 16
        B, S, H = x.shape
        nh = NUM_HEADS
        hd = H // nh
        attn_scale = 1.0 / np.sqrt(hd).astype(np.float32)
        qkv = x @ w_qkv + b_qkv
        q, k, v = jnp.split(qkv, 3, axis=-1)
        to_heads = lambda t: t.reshape(B, S, nh, hd).transpose(0, 2, 1, 3)
        q, k, v = (to_heads(q), to_heads(k), to_heads(v))
        scores = jnp.einsum('bhid,bhjd->bhij', q, k) * attn_scale
        i = jnp.arange(S)[:, None]
        j = jnp.arange(S)[None, :]
        scores = jnp.where(j >= i, scores, -jnp.inf)
        attn = jax.nn.softmax(scores, axis=-1)
        out = jnp.einsum('bhij,bhjd->bhid', attn, v)
        out = out.transpose(0, 2, 1, 3).reshape(B, S, H)
        return out @ w_out + b_out

    def _L0_xattn_ref(q, k, v, W_proj, b_proj):
        import jax, jax.numpy as jnp
        import numpy as np
        B, T, N_EMBD, N_HEAD = (2, 512, 256, 16)
        HEAD = N_EMBD // N_HEAD
        WINDOW = 64
        Bsz, Tlen, _ = q.shape
        qh = q.reshape(Bsz, Tlen, N_HEAD, HEAD).transpose(0, 2, 1, 3)
        kh = k.reshape(Bsz, Tlen, N_HEAD, HEAD).transpose(0, 2, 1, 3)
        vh = v.reshape(Bsz, Tlen, N_HEAD, HEAD).transpose(0, 2, 1, 3)
        scale = 1.0 / np.sqrt(HEAD)
        scores = jnp.einsum('bhqd,bhkd->bhqk', qh, kh) * scale
        idx = jnp.arange(Tlen)
        dist = jnp.abs(idx[None, :] - idx[:, None])
        scores = jnp.where(dist[None, None] > WINDOW, -jnp.inf, scores)
        attn = jax.nn.softmax(scores, axis=-1)
        y = jnp.einsum('bhqk,bhkd->bhqd', attn, vh)
        y = y.transpose(0, 2, 1, 3).reshape(Bsz, Tlen, N_EMBD)
        return y @ W_proj.T + b_proj

    def _L0_ffn_ref(x, gate_w, Wu, Wv, Wo):
        import jax, jax.numpy as jnp
        import numpy as np
        B, N, D, E, R, K = (4, 512, 256, 8, 64, 2)
        logits = jnp.einsum('bnd,de->bne', x, gate_w)
        topv, topi = jax.lax.top_k(logits, K)
        w = jax.nn.softmax(topv, axis=-1)
        u = jnp.einsum('bnd,edr->bner', x, Wu)
        v = jnp.einsum('bnd,edr->bner', x, Wv)
        s = jax.nn.silu(u) * v
        Y = jnp.einsum('bner,erd->bned', s, Wo)
        y_sel = jnp.take_along_axis(Y, topi[..., None], axis=2)
        out = jnp.einsum('bnkd,bnk->bnd', y_sel, w)
        return out
    x = _layernorm(x + _L0_attn_ref(x, L0_attn_w_qkv, L0_attn_b_qkv, L0_attn_w_out, L0_attn_b_out), axis=-1)
    x = _layernorm(x + _L0_xattn_ref(x, ctx_1024, ctx_1024, L0_xattn_W_proj, L0_xattn_b_proj), axis=-1)
    x = _layernorm(x + _L0_ffn_ref(x, L0_ffn_gate_w, L0_ffn_Wu, L0_ffn_Wv, L0_ffn_Wo), axis=-1)
    return x

_drawn_inputs = setup_inputs


def setup_inputs(seed=0):
    import zlib

    import numpy as np

    out = dict(_drawn_inputs(seed))
    spreads = {'L0_xattn_b_proj': (0.0, 0.1)}
    factors = {'L0_attn_w_qkv': 2.914,
     'L0_attn_b_qkv': 8.0,
     'L0_attn_w_out': 2.805,
     'L0_attn_b_out': 3.216,
     'L0_ffn_gate_w': 8.0,
     'L0_ffn_Wu': 8.0,
     'L0_ffn_Wv': 8.0,
     'L0_ffn_Wo': 8.0}
    for name, (base, spread) in spreads.items():
        noise = np.random.default_rng([zlib.crc32(name.encode()), seed]).standard_normal(out[name].shape)
        drawn = base * np.exp(spread * noise) if base else spread * noise
        out[name] = jnp.asarray(drawn.astype(out[name].dtype))
    for name, factor in factors.items():
        out[name] = (out[name] * factor).astype(out[name].dtype)
    return out
```

```python
from contextlib import ExitStack

import concourse.bass as bass
from concourse import mybir

ALU = mybir.AluOpType
ACT = mybir.ActivationFunctionType
F32 = mybir.dt.float32
BF16 = mybir.dt.bfloat16
U32 = mybir.dt.uint32
AX_X = mybir.AxisListType.X

P = 128
D = 256
KT = D // P
HEADS, HD = 16, 16
UNITS = 4
HPU = HEADS // UNITS
VW = 32
E, R = 8, 64
FT = E * R // P
TERMS = 6
KS = TERMS * HD
Q_PARTS = (0, 0, 0, 1, 1, 2)
K_PARTS = (0, 1, 2, 0, 1, 0)
UNROLL = 4
EPS = 1e-5
SCALE = HD ** -0.5

A1, A2 = 3, 6
X1T, POST2 = A1 + 1, A2 + 1
GATE = A2 + 2
FUP = 9
Y = 10


class Slot:

    def __init__(self, turn, off):
        self.turn, self.off = turn, off

    def behind(self, lag):
        return Slot(self.turn, self.off - lag)

    def at(self, per, more):
        return self.turn * (UNROLL * per) + (self.off * per + more)

    def group_at(self, per, more):
        return self.turn * (UNROLL // 2 * per) + (self.off // 2 * per + more)

    def use_at(self, per, more):
        return self.turn * per + (self.off // 4 * per + more)

    def exists(self, n):
        return not isinstance(self.turn, int) or 0 <= UNROLL * self.turn + self.off < n


def due(count):
    return not isinstance(count, int) or count > 0


def in_register(eng, count):
    return count if isinstance(count, int) else eng.to_reg(count)


def decoder_layer(nc, x, xT, ctx_tok, ctxT, w_qkv, b_qk, b_v, w_out, b_out, w_proj, b_proj,
                  gate_w, w_u, w_v, w_o, ident, ident_bf, masks, head_sel, expert_sel, iota8, out):
    NB = x.shape[0]
    NG = NB // 2
    LAST = Y + 2
    assert NB % UNROLL == 0 and LAST % UNROLL == 0

    with ExitStack() as ctx:
        def sb(name, shape, dt=F32):
            return ctx.enter_context(nc.sbuf_tensor(name, shape, dt))

        def sem(name):
            return ctx.enter_context(nc.semaphore(name))

        wqkv_sb = sb("wqkv_sb", [P, KT, 3 * D])
        bqk_sb = sb("bqk_sb", [P, 4])
        bv_sb = sb("bv_sb", [P, D])
        wout_sb = sb("wout_sb", [P, KT, D])
        bout_sb = sb("bout_sb", [P, D])
        wproj_sb = sb("wproj_sb", [P, KT, D])
        bproj_sb = sb("bproj_sb", [P, D])
        gatew_sb = sb("gatew_sb", [P, KT, E])
        wu_sb = sb("wu_sb", [P, KT, E * R])
        wv_sb = sb("wv_sb", [P, KT, E * R])
        wo_sb = sb("wo_sb", [P, FT, D])
        ident_f = sb("ident_f", [P, P])
        ident_b = sb("ident_b", [P, P], BF16)
        mask_sb = sb("mask_sb", [P, 2, P], BF16)
        headsel_sb = sb("headsel_sb", [2 * HEADS, HEADS, P], BF16)
        expsel_sb = sb("expsel_sb", [3 * E, FT, P], BF16)
        iota_sb = sb("iota_sb", [P, E])
        mhalf = sb("mhalf", [P, 1])

        xT_sb = sb("xT_sb", [P, 2, KT, 2 * P])
        xtok_sb = sb("xtok_sb", [P, 2, 2, D])
        ctxT_sb = sb("ctxT_sb", [P, 2, KT, 2 * P])
        ctxtok_sb = sb("ctxtok_sb", [P, 2, 2, D])
        part = {n: sb(f"part_{n}", [P, 3, KT, 2 * P], BF16) for n in ("q", "k", "x1", "ctx")}
        rest = {n: sb(f"rest_{n}", [P, KT, 2 * P]) for n in ("q", "k", "x1", "ctx")}
        stack = {n: sb(f"stack_{n}", [KS, 2, HEADS, 2 * P], BF16) for n in ("q", "k", "x1", "ctx")}
        val1 = sb("val1", [P, 4, HEADS, VW])
        val2 = sb("val2", [P, 4, HEADS, VW])
        negmax = [sb(f"negmax{i}", [P, HEADS]) for i in (1, 2)]
        negmax_hl = [sb(f"negmax_hl{i}", [P, 2, HEADS], BF16) for i in (1, 2)]
        negmax_T = [sb(f"negmax_T{i}", [2 * HEADS, P], BF16) for i in (1, 2)]
        probs = sb("probs", [P, UNITS, HPU, P])
        o_sb = [sb(f"o_sb{i}", [P, UNITS, P]) for i in (1, 2)]
        rden = [sb(f"rden{i}", [P, HEADS]) for i in (1, 2)]
        att = [sb(f"att{i}", [P, HEADS, HD]) for i in (1, 2)]
        attT = [sb(f"attT{i}", [P, KT, P]) for i in (1, 2)]
        z = [sb(f"z{i}", [P, D]) for i in (1, 2, 3)]
        stats = [sb(f"stats{i}", [P, 6]) for i in (1, 2, 3)]
        meanvar = [sb(f"meanvar{i}", [P, 2]) for i in (1, 2, 3)]
        vareps = [sb(f"vareps{i}", [P, 1]) for i in (1, 2, 3)]
        rstd = [sb(f"rstd{i}", [P, 1]) for i in (1, 2, 3)]
        x1 = sb("x1", [P, 4, D])
        x1b = sb("x1b", [P, 4, D])
        x2 = sb("x2", [P, 4, D])
        x2T = sb("x2T", [P, 2, KT, 2 * P])
        logit = sb("logit", [P, E])
        top8 = sb("top8", [P, 8])
        topi = sb("topi", [P, 8], U32)
        topf = sb("topf", [P, 2])
        first = sb("first", [P, E])
        chosen = sb("chosen", [P, E])
        below = sb("below", [P, E])
        gexp = sb("gexp", [P, E])
        gsel = sb("gsel", [P, E])
        gsum = sb("gsum", [P, 1])
        ginv = sb("ginv", [P, 1])
        gate = sb("gate", [P, E])
        gate_r = sb("gate_r", [P, E])
        gate_parts = sb("gate_parts", [P, 3, E], BF16)
        gateT = sb("gateT", [3 * E, 2, 2 * P], BF16)
        th = sb("th", [P, 2, 2 * P])
        silu = sb("silu", [P, 2, 2 * P])
        prod = sb("prod", [P, 2, 2 * P])
        hid = sb("hid", [P, 2, FT, 2 * P])
        y_sb = sb("y_sb", [P, 2, D])

        bank_s = [ctx.enter_context(nc.psum_tensor(f"bank_s{i}", [P, 512], F32)) for i in range(2)]
        bank_t = [ctx.enter_context(nc.psum_tensor(f"bank_t{i}", [P, 512], F32)) for i in range(2)]
        bank_o = ctx.enter_context(nc.psum_tensor("bank_o", [P, 512], F32))
        bank_x = ctx.enter_context(nc.psum_tensor("bank_x", [P, 512], F32))
        bank_l = [ctx.enter_context(nc.psum_tensor(f"bank_l{i}", [P, 512], F32)) for i in range(2)]

        consts_in = sem("consts_in")
        const_set = sem("const_set")
        xT_in = [sem(f"xT_in{i}") for i in range(2)]
        xtok_in = [sem(f"xtok_in{i}") for i in range(2)]
        ctxT_in = [sem(f"ctxT_in{i}") for i in range(2)]
        ctxtok_in = [sem(f"ctxtok_in{i}") for i in range(2)]
        stacked = {n: [sem(f"stacked_{n}{i}") for i in range(2)] for n in stack}
        out_written = [sem(f"out_written{i}") for i in range(2)]
        qk_psum = sem("qk_psum")
        v_psum = sem("v_psum")
        qk_head = sem("qk_head")
        qk_rest = sem("qk_rest")
        v_out = sem("v_out")
        part1 = {n: sem(f"part1_{n}") for n in ("ctx", "x1")}
        rest1 = {n: sem(f"rest1_{n}") for n in ("ctx", "x1")}
        part2 = {n: sem(f"part2_{n}") for n in part}
        part3 = {n: sem(f"part3_{n}") for n in part}
        xb_ready = sem("xb_ready")
        val2_ready = sem("val2_ready")
        scores = [sem(f"scores{i}") for i in (1, 2)]
        maxed = [sem(f"maxed{i}") for i in (1, 2)]
        max_hi = [sem(f"max_hi{i}") for i in (1, 2)]
        max_lo = [sem(f"max_lo{i}") for i in (1, 2)]
        maxT_psum = [sem(f"maxT_psum{i}") for i in (1, 2)]
        maxT_out = [sem(f"maxT_out{i}") for i in (1, 2)]
        scoresT = [sem(f"scoresT{i}") for i in (1, 2)]
        exped = [sem(f"exped{i}") for i in (1, 2)]
        masked = [sem(f"masked{i}") for i in (1, 2)]
        pv_done = [sem(f"pv_done{i}") for i in (1, 2)]
        o_out = [sem(f"o_out{i}") for i in (1, 2)]
        tok_psum = [sem(f"tok_psum{i}") for i in (1, 2)]
        recip_done = [sem(f"recip_done{i}") for i in (1, 2)]
        normed = [sem(f"normed{i}") for i in (1, 2)]
        attT_psum = [sem(f"attT_psum{i}") for i in (1, 2)]
        attT_out = [sem(f"attT_out{i}") for i in (1, 2)]
        proj_psum = [sem(f"proj_psum{i}") for i in (1, 2)]
        summed = [sem(f"summed{i}") for i in (1, 2, 3)]
        stats_out = [sem(f"stats_out{i}") for i in (1, 2, 3)]
        mv_out = [sem(f"mv_out{i}") for i in (1, 2, 3)]
        vareps_out = [sem(f"vareps_out{i}") for i in (1, 2, 3)]
        rstd_out = [sem(f"rstd_out{i}") for i in (1, 2, 3)]
        ln_out = [sem(f"ln_out{i}") for i in (1, 2, 3)]
        x1b_ready = sem("x1b_ready")
        x1T_psum = sem("x1T_psum")
        x2T_psum = sem("x2T_psum")
        x2T_out = sem("x2T_out")
        logit_psum = sem("logit_psum")
        gate_step = sem("gate_step")
        gexp_out = sem("gexp_out")
        gate_rest = sem("gate_rest")
        gateT_psum = sem("gateT_psum")
        gateT_out = sem("gateT_out")
        uv_psum = sem("uv_psum")
        g_psum = sem("g_psum")
        tanh_out = sem("tanh_out")
        silu_out = sem("silu_out")
        prod_out = sem("prod_out")
        hid_out = sem("hid_out")
        y_psum = sem("y_psum")
        GATE_STEPS = 14

        def other_so_far(i, k, per):
            if i == 0:
                o = k.behind(A2 - A1 + 1)
                if not o.exists(NB):
                    return 0
                return o.at(per, per)
            o = k.behind(A1 - A2)
            if not o.exists(NB):
                return per * NB
            return o.at(per, per)

        block = ctx.enter_context(nc.Block())

        def run(eng, slot_program):
            for s in range(LAST):
                slot_program(Slot(s // UNROLL, s % UNROLL))
            with eng.Fori(LAST // UNROLL, NB // UNROLL - 1) as turn:
                for j in range(UNROLL):
                    slot_program(Slot(turn, j))
            for s in range(NB - UNROLL, NB + LAST):
                slot_program(Slot(s // UNROLL, s % UNROLL))

        @block.sync
        def _(sp):
            loads = [
                (wqkv_sb[:], w_qkv.rearrange("(k p) n -> p k n", p=P)),
                (bqk_sb[:], b_qk), (bv_sb[:], b_v.partition_broadcast(P)),
                (ident_f[:], ident), (ident_b[:], ident_bf), (iota_sb[:], iota8.partition_broadcast(P)),
                (wout_sb[:], w_out.rearrange("(k p) n -> p k n", p=P)),
                (bout_sb[:], b_out.partition_broadcast(P)),
                (wproj_sb[:], w_proj.rearrange("(k p) n -> p k n", p=P)),
                (bproj_sb[:], b_proj.partition_broadcast(P)),
                (gatew_sb[:], gate_w.rearrange("(k p) n -> p k n", p=P)),
                (wu_sb[:], w_u.rearrange("(k p) n -> p k n", p=P)),
                (wv_sb[:], w_v.rearrange("(k p) n -> p k n", p=P)),
                (wo_sb[:], w_o.rearrange("(k p) n -> p k n", p=P)),
                (mask_sb[:], masks), (headsel_sb[:], head_sel), (expsel_sb[:], expert_sel),
            ]
            for dst, src in loads:
                sp.dma_start(dst, src).then_inc(consts_in, 16)

            def load_xT(k):
                if due(count := k.at(1, 2 - 4)):
                    sp.wait_ge(v_psum, count)
                sp.dma_start(xT_sb[:, k.off // 2 % 2], xT[k.group_at(1, 0)])\
                    .then_inc(xT_in[k.off // 2 % 2], 16)

            def slot(s):
                even = s.off % 2 == 0
                k = s.behind(-2)
                if even and k.exists(NB):
                    load_xT(k)
                k = s.behind(2)
                if even and k.exists(NB):
                    if due(count := k.at(1, 2 - 4)):
                        sp.wait_ge(summed[0], count)
                    sp.dma_start(xtok_sb[:, k.off // 2 % 2], x[bass.ds(k.at(1, 0), 2)].rearrange("b s d -> s b d"))\
                        .then_inc(xtok_in[k.off // 2 % 2], 16)
                k = s.behind(2)
                if even and k.exists(NB):
                    if due(count := k.group_at(1, 1 - 2)):
                        sp.wait_ge(part1["ctx"], count)
                    if due(count := k.group_at(1, 1 - 2)):
                        sp.wait_ge(rest1["ctx"], count)
                    sp.dma_start(ctxT_sb[:, k.off // 2 % 2], ctxT[k.group_at(1, 0)])\
                        .then_inc(ctxT_in[k.off // 2 % 2], 16)
                    if due(count := k.at(1, 2 - 4)):
                        sp.wait_ge(val2_ready, count)
                    sp.dma_start(ctxtok_sb[:, k.off // 2 % 2], ctx_tok[bass.ds(k.at(1, 0), 2)].rearrange("b s d -> s b d"))\
                        .then_inc(ctxtok_in[k.off // 2 % 2], 16)

                def stack_up(name, k, parts, readers):
                    if due(count := k.at(UNITS, UNITS * (2 - 4))):
                        sp.wait_ge(readers, count)
                    sp.wait_ge(part2[name], k.group_at(1, 1))
                    sp.wait_ge(part3[name], k.group_at(1, 1))
                    ring = k.off // 2 % 2
                    for c in range(TERMS):
                        dst = stack[name][HD * c:HD * c + HD, ring].rearrange("p (a t) n -> p a t n", t=2)
                        sp.dma_start(dst, part[name][:, parts[c]]).then_inc(stacked[name][ring], 16)

                k = s.behind(1)
                if not even and k.exists(NB):
                    stack_up("q", k, Q_PARTS, scoresT[0])
                k = s.behind(2)
                if even and k.exists(NB):
                    stack_up("k", k, K_PARTS, scoresT[0])
                k = s.behind(4)
                if even and k.exists(NB):
                    stack_up("ctx", k, K_PARTS, scoresT[1])
                k = s.behind(5)
                if not even and k.exists(NB):
                    stack_up("x1", k, Q_PARTS, scoresT[1])
                k = s.behind(Y + 1)
                if k.exists(NB):
                    sp.wait_ge(ln_out[2], k.at(1, 1))
                    sp.dma_start(out[k.at(1, 0)], y_sb[:, k.off % 2]).then_inc(out_written[k.off % 2], 16)

            load_xT(Slot(0, 0))
            run(sp, slot)
            for i in range(2):
                sp.wait_ge(out_written[i], 16 * NB // 2)

        @block.tensor
        def _(pe):
            pe.wait_ge(consts_in, 16 * 17)

            def score_pass(i, k, q, kk, ring):
                b = k.off % 2 * P
                if k.off % 2 == 0:
                    pe.wait_ge(stacked[q][ring], k.use_at(16 * TERMS, 16 * TERMS))
                    pe.wait_ge(stacked[kk][ring], k.use_at(16 * TERMS, 16 * TERMS))
                for u in range(UNITS):
                    if u == 0:
                        if due(count := other_so_far(i, k, 1)):
                            pe.wait_ge(maxT_out[1 - i], count)
                        if due(count := other_so_far(i, k, UNITS)):
                            pe.wait_ge(maxed[1 - i], count)
                    if u >= 2:
                        if due(count := k.at(UNITS, u - 1)):
                            pe.wait_ge(maxed[i], count)
                    bank = bank_s[u % 2]
                    pe.matmul(bank[:], ident_b[:], mask_sb[:, i, None, :].broadcast_to([P, HPU, P]),
                              start=True, stop=False, skip_group_check=True)
                    for a in range(HPU):
                        h = HPU * u + a
                        mm = pe.matmul(bank[:, a * P:(a + 1) * P], stack[q][:, ring, h, b:b + P],
                                       stack[kk][:, ring, h, b:b + P], start=False, stop=(a == HPU - 1),
                                       skip_group_check=True)
                    mm.then_inc(scores[i], 1)

            def max_transpose(i, k):
                pe.wait_ge(max_lo[i], k.at(1, 1))
                pe.transpose(bank_s[0].bitcast(BF16)[0:2 * HEADS, 0:P],
                             negmax_hl[i][:].rearrange("p c h -> p (c h)"), ident_b[:])\
                    .then_inc(maxT_psum[i], 1)

            def attend(i, k, q, kk, ring, val):
                b = k.off % 2 * P

                def scores_T(u):
                    if u >= 2:
                        if due(count := k.at(UNITS, u - 1)):
                            pe.wait_ge(exped[i], count)
                    bank = bank_t[u % 2]
                    for a in range(HPU):
                        h = HPU * u + a
                        pe.matmul(bank[:, a * P:(a + 1) * P], stack[kk][:, ring, h, b:b + P],
                                  stack[q][:, ring, h, b:b + P], start=True, stop=False, skip_group_check=True)
                        mm = pe.matmul(bank[:, a * P:(a + 1) * P], headsel_sb[:, h, :], negmax_T[i][:],
                                       start=False, stop=True, skip_group_check=True)
                    mm.then_inc(scoresT[i], 1)

                def weigh(u):
                    pe.wait_ge(masked[i], k.at(UNITS, u + 1))
                    for a in range(HPU):
                        h = HPU * u + a
                        mm = pe.matmul(bank_o[VW * a:VW * a + VW, u * P:(u + 1) * P],
                                       val[:, k.off % 4, h, :], probs[:, u, a, :], start=True, stop=True,
                                       tile_position=(0, VW * a))
                    mm.then_inc(pv_done[i], 1)

                pe.wait_ge(maxT_out[i], k.at(1, 1))
                if due(count := other_so_far(i, k, UNITS)):
                    pe.wait_ge(exped[1 - i], count)
                scores_T(0)
                scores_T(1)
                if i == 0:
                    pe.wait_ge(v_out, k.at(1, 1))
                    o = k.behind(A2 - A1 + 1)
                    if o.exists(NB):
                        pe.wait_ge(normed[1], o.at(1, 1))
                else:
                    pe.wait_ge(val2_ready, k.at(1, 1))
                    o = k.behind(A1 - A2)
                    if o.exists(NB):
                        pe.wait_ge(normed[0], o.at(1, 1))
                    f = k.behind(FUP - A2)
                    if f.exists(NB):
                        pe.wait_ge(hid_out, f.at(2, 2))
                for u in range(UNITS):
                    if u + 2 < UNITS:
                        scores_T(u + 2)
                    weigh(u)

            def tokens(i, k):
                pe.wait_ge(o_out[i], k.at(1, 1))
                for u in range(UNITS):
                    mm = pe.transpose(bank_o[:, u * P:(u + 1) * P], o_sb[i][:, u, :], ident_f[:])
                mm.then_inc(tok_psum[i], 1)

            def att_transpose(i, k):
                pe.wait_ge(normed[i], k.at(1, 1))
                for t in range(KT):
                    mm = pe.transpose(bank_x[:, t * P:(t + 1) * P],
                                      att[i][:].rearrange("p h d -> p (h d)")[:, t * P:(t + 1) * P], ident_f[:])
                mm.then_inc(attT_psum[i], 1)

            def project(i, k, w):
                pe.wait_ge(attT_out[i], k.at(1, 1))
                for t in range(KT):
                    mm = pe.matmul(bank_l[1][:, 0:D], attT[i][:, t, :], w[:, t, :], start=(t == 0), stop=(t == KT - 1))
                mm.then_inc(proj_psum[i], 1)

            def slot(s):
                even = s.off % 2 == 0
                k = s.behind(A1)
                if k.exists(NB):
                    score_pass(0, k, "q", "k", k.off // 2 % 2)
                k = s.behind(GATE)
                if k.exists(NB):
                    pe.wait_ge(x2T_out, k.at(1, 1))
                    o = s.behind(1 + A1)
                    if o.exists(NB):
                        pe.wait_ge(summed[0], o.at(1, 1))
                    elif s.behind(1 + FUP).exists(NB):
                        pe.wait_ge(prod_out, s.behind(1 + FUP).at(2, 2))
                    g, b = k.off // 2 % 2, k.off % 2 * P
                    for t in range(KT):
                        mm = pe.matmul(bank_l[1][:, 0:E], x2T[:, g, t, b:b + P], gatew_sb[:, t, :],
                                       start=(t == 0), stop=(t == KT - 1))
                    mm.then_inc(logit_psum, 1)
                k = s.behind(X1T)
                if k.exists(NB):
                    pe.wait_ge(ln_out[0], k.at(1, 1))
                    o = s.behind(1 + POST2)
                    if o.exists(NB):
                        pe.wait_ge(x2T_out, o.at(1, 1))
                    for t in range(KT):
                        mm = pe.transpose(bank_x[:, t * P:(t + 1) * P],
                                          x1[:, k.off % 4, t * P:(t + 1) * P],
                                          ident_f[:])
                    mm.then_inc(x1T_psum, 1)
                k = s.behind(POST2)
                if k.exists(NB):
                    tokens(1, k)
                k = s
                if k.exists(NB):
                    ring, b = k.off // 2 % 2, k.off % 2
                    if even:
                        pe.wait_ge(xT_in[ring], k.use_at(16, 16))
                    o = s.behind(1 + Y)
                    if o.exists(NB):
                        pe.wait_ge(summed[2], o.at(1, 1))
                    else:
                        if due(count := s.at(1, 0)):
                            pe.wait_ge(qk_rest, count)
                        if s.behind(1 + FUP).exists(NB):
                            pe.wait_ge(prod_out, s.behind(1 + FUP).at(2, 1))
                    for t in range(2):
                        for c in range(KT):
                            mm = pe.matmul(bank_l[0][:, t * 2 * P:(t + 1) * 2 * P],
                                           wqkv_sb[:, c, (2 * b + t) * P:(2 * b + t + 1) * P], xT_sb[:, ring, c, :],
                                           start=(c == 0), stop=(c == KT - 1))
                    mm.then_inc(qk_psum, 1)
                    o = s.behind(1 + A1)
                    if o.exists(NB):
                        pe.wait_ge(summed[0], o.at(1, 1))
                    if due(count := s.at(1, 0)):
                        pe.wait_ge(v_out, count)
                    o = s.behind(GATE)
                    if o.exists(NB):
                        pe.wait_ge(gate_step, o.at(GATE_STEPS, 1))
                    for c in range(KT):
                        mm = pe.matmul(bank_l[1][:, 0:D], xT_sb[:, ring, c, b * P:(b + 1) * P],
                                       wqkv_sb[:, c, 2 * D:3 * D], start=(c == 0), stop=(c == KT - 1))
                    mm.then_inc(v_psum, 1)
                k = s.behind(A1)
                if k.exists(NB):
                    max_transpose(0, k)
                k = s.behind(POST2)
                if k.exists(NB):
                    o = s.behind(X1T)
                    if o.exists(NB):
                        pe.wait_ge(rest1["x1"], o.at(1, 1))
                    else:
                        pe.wait_ge(rest1["x1"], NB)
                    if due(count := k.at(1, 0)):
                        pe.wait_ge(x2T_out, count)
                    att_transpose(1, k)
                k = s.behind(GATE)
                if k.exists(NB):
                    pe.wait_ge(gate_step, k.at(GATE_STEPS, GATE_STEPS))
                    o = s.behind(POST2)
                    if o.exists(NB):
                        pe.wait_ge(attT_out[1], o.at(1, 1))
                    pe.transpose(bank_x.bitcast(BF16)[0:3 * E, 0:P],
                                 gate_parts[:].rearrange("p c e -> p (c e)"), ident_b[:]).then_inc(gateT_psum, 1)
                k = s.behind(A1)
                if k.exists(NB):
                    attend(0, k, "q", "k", k.off // 2 % 2, val1)
                k = s.behind(POST2)
                if k.exists(NB):
                    if s.exists(NB):
                        pe.wait_ge(v_out, s.at(1, 1))
                    else:
                        pe.wait_ge(gate_step, s.behind(GATE).at(GATE_STEPS, 1))
                    project(1, k, wproj_sb)
                k = s.behind(A2)
                if k.exists(NB):
                    score_pass(1, k, "x1", "ctx", k.off // 2 % 2)
                k = s.behind(A1)
                if k.exists(NB):
                    tokens(0, k)
                k = s.behind(FUP)
                if k.exists(NB):
                    ring, half = k.off // 2 % 2, k.off % 2
                    for f in range(2):
                        ft = 2 * half + f
                        if f == 0:
                            if s.exists(NB):
                                pe.wait_ge(qk_rest, s.at(1, 1))
                            else:
                                pe.wait_ge(summed[2], s.behind(1 + Y).at(1, 1))
                            if half == 0:
                                pe.wait_ge(x2T_out, k.at(1, 2))
                        else:
                            o = s.behind(POST2)
                            if o.exists(NB):
                                pe.wait_ge(summed[1], o.at(1, 1))
                            elif s.behind(GATE).exists(NB):
                                pe.wait_ge(gate_step, s.behind(GATE).at(GATE_STEPS, 1))
                            else:
                                if due(count := k.at(2, 0)):
                                    pe.wait_ge(prod_out, count)
                        for n, w in enumerate((wu_sb, wv_sb)):
                            for c in range(KT):
                                mm = pe.matmul(bank_l[f][:, n * 2 * P:(n + 1) * 2 * P],
                                               w[:, c, ft * P:(ft + 1) * P], x2T[:, ring, c, :],
                                               start=(c == 0), stop=(c == KT - 1))
                        mm.then_inc(uv_psum, 1)
                    if half == 0:
                        pe.wait_ge(gateT_out, k.at(1, 2))
                    o = s.behind(A1)
                    pe.wait_ge(normed[0], o.at(1, 1) if o.exists(NB) else NB)
                    pe.wait_ge(normed[1], s.behind(POST2).at(1, 1) if s.behind(POST2).exists(NB) else NB)
                    for f in range(2):
                        mm = pe.matmul(bank_o[:, f * 2 * P:(f + 1) * 2 * P], expsel_sb[:, 2 * half + f, :],
                                       gateT[:, ring, :], start=True, stop=True)
                    mm.then_inc(g_psum, 1)
                k = s.behind(A2)
                if k.exists(NB):
                    max_transpose(1, k)
                k = s.behind(A1)
                if k.exists(NB):
                    o = s.behind(GATE)
                    if o.exists(NB):
                        pe.wait_ge(gateT_out, o.at(1, 1))
                    if s.behind(POST2).exists(NB):
                        pe.wait_ge(attT_out[1], s.behind(POST2).at(1, 1))
                    if s.behind(X1T).exists(NB):
                        pe.wait_ge(rest1["x1"], s.behind(X1T).at(1, 1))
                    att_transpose(0, k)
                k = s.behind(A2)
                if k.exists(NB):
                    attend(1, k, "x1", "ctx", k.off // 2 % 2, val2)
                k = s.behind(A1)
                if k.exists(NB):
                    o = s.behind(FUP)
                    if o.exists(NB):
                        pe.wait_ge(prod_out, o.at(2, 2))
                    if s.behind(POST2).exists(NB):
                        pe.wait_ge(summed[1], s.behind(POST2).at(1, 1))
                    if s.exists(NB):
                        pe.wait_ge(v_out, s.at(1, 1))
                    project(0, k, wout_sb)
                k = s.behind(POST2)
                if k.exists(NB):
                    pe.wait_ge(ln_out[1], k.at(1, 1))
                    o = s.behind(A1)
                    pe.wait_ge(attT_out[0], o.at(1, 1) if o.exists(NB) else NB)
                    if s.behind(GATE).exists(NB):
                        pe.wait_ge(gateT_out, s.behind(GATE).at(1, 1))
                    pe.wait_ge(attT_out[1], k.at(1, 1))
                    for t in range(KT):
                        mm = pe.transpose(bank_x[:, t * P:(t + 1) * P],
                                          x2[:, k.off % 4, t * P:(t + 1) * P], ident_f[:])
                    mm.then_inc(x2T_psum, 1)
                k = s.behind(Y)
                if k.exists(NB):
                    ring, b = k.off // 2 % 2, k.off % 2
                    if b == 0:
                        pe.wait_ge(hid_out, k.at(2, 4))
                    o = s.behind(FUP)
                    pe.wait_ge(prod_out, o.at(2, 1) if o.exists(NB) else 2 * NB)
                    if not o.exists(NB):
                        if due(count := k.at(1, 0)):
                            pe.wait_ge(summed[2], count)
                    for f in range(FT):
                        mm = pe.matmul(bank_l[0][:, 0:D], hid[:, ring, f, b * P:(b + 1) * P], wo_sb[:, f, :],
                                       start=(f == 0), stop=(f == FT - 1))
                    mm.then_inc(y_psum, 1)

            run(pe, slot)

        @block.scalar
        def _(act):
            act.wait_ge(consts_in, 16 * 17)

            def exponentials(i, k):
                for u in range(UNITS):
                    act.wait_ge(scoresT[i], k.at(UNITS, u + 1))
                    if u == 0:
                        if due(count := other_so_far(i, k, UNITS)):
                            act.wait_ge(pv_done[1 - i], count)
                    act.activation(probs[:, u].rearrange("p a n -> p (a n)"), bank_t[u % 2][:],
                                   ACT.Exp, scale=SCALE).then_inc(exped[i], 1)
                act.wait_ge(pv_done[i], k.at(UNITS, UNITS))
                if due(count := k.at(1, 0)):
                    act.wait_ge(tok_psum[i], count)
                act.copy(o_sb[i][:].rearrange("p u n -> p (u n)"), bank_o[:]).then_inc(o_out[i], 1)

            def max_out(i, k):
                act.wait_ge(maxT_psum[i], k.at(1, 1))
                if due(count := k.at(UNITS, 0)):
                    act.wait_ge(scoresT[i], count)
                act.copy(negmax_T[i][:], bank_s[0].bitcast(BF16)[0:2 * HEADS, 0:P]).then_inc(maxT_out[i], 1)

            def att_out(i, k):
                act.wait_ge(attT_psum[i], k.at(1, 1))
                if due(count := k.at(1, 0)):
                    act.wait_ge(proj_psum[i], count)
                act.copy(attT[i][:].rearrange("p t n -> p (t n)"), bank_x[:, 0:D]).then_inc(attT_out[i], 1)

            def slot(s):
                even = s.off % 2 == 0
                k = s.behind(X1T)
                if k.exists(NB):
                    b = k.off % 2 * P
                    act.wait_ge(x1T_psum, k.at(1, 1))
                    ring = (k.off // 2 - 1) % 2
                    if due(count := k.behind(2).use_at(16 * TERMS, 16 * TERMS) if k.behind(2).exists(NB) else 0):
                        act.wait_ge(stacked["x1"][ring], count)
                    act.copy(part["x1"][:, 0, :, b:b + P], bank_x[:, 0:D].rearrange("p (t n) -> p t n", t=2))\
                        .then_inc(part1["x1"], 1)
                k = s.behind(GATE)
                if k.exists(NB):
                    act.wait_ge(gate_step, k.at(GATE_STEPS, 7))
                    act.activation(gexp[:], below[:], ACT.Exp).then_inc(gexp_out, 1)
                k = s
                if k.exists(NB):
                    name = "q" if even else "k"
                    act.wait_ge(qk_psum, k.at(1, 1))
                    ring = (k.off // 2 - 1) % 2
                    if due(count := k.behind(2).use_at(16 * TERMS, 16 * TERMS) if k.behind(2).exists(NB) else 0):
                        act.wait_ge(stacked[name][ring], count)
                    for t in range(2):
                        op = act.activation(part[name][:, 0, t, :], bank_l[0][:, t * 2 * P:(t + 1) * 2 * P],
                                            ACT.Identity, bias=bqk_sb[:, 2 * (not even) + t:2 * (not even) + t + 1])
                    op.then_inc(qk_head, 1)
                k = s.behind(3)
                if not even and k.exists(NB):
                    ring = k.off // 2 % 2
                    act.wait_ge(ctxT_in[ring], k.use_at(16, 16))
                    if due(count := k.behind(2).use_at(16 * TERMS, 16 * TERMS) if k.behind(2).exists(NB) else 0):
                        act.wait_ge(stacked["ctx"][1 - ring], count)
                    act.copy(part["ctx"][:, 0], ctxT_sb[:, ring]).then_inc(part1["ctx"], 1)
                k = s.behind(A1)
                if k.exists(NB):
                    max_out(0, k)
                k = s.behind(POST2)
                if k.exists(NB):
                    att_out(1, k)
                k = s.behind(GATE)
                if k.exists(NB):
                    act.wait_ge(gateT_psum, k.at(1, 1))
                    if due(count := k.at(1, k.off // 2 * 2 - k.off - 2)):
                        act.wait_ge(g_psum, count)
                    act.copy(gateT[:, k.off // 2 % 2, k.off % 2 * P:(k.off % 2 + 1) * P],
                             bank_x.bitcast(BF16)[0:3 * E, 0:P]).then_inc(gateT_out, 1)
                k = s.behind(A1)
                if k.exists(NB):
                    exponentials(0, k)
                k = s.behind(FUP)
                if k.exists(NB):
                    for f in range(2):
                        act.wait_ge(uv_psum, k.at(2, f + 1))
                        if due(count := k.at(2, f - 1)):
                            act.wait_ge(silu_out, count)
                        act.activation(th[:, f, :], bank_l[f][:, 0:2 * P], ACT.Tanh, scale=0.5)\
                            .then_inc(tanh_out, 1)
                k = s.behind(A2)
                if k.exists(NB):
                    max_out(1, k)
                k = s.behind(A1)
                if k.exists(NB):
                    att_out(0, k)
                k = s.behind(A2)
                if k.exists(NB):
                    exponentials(1, k)
                k = s.behind(POST2)
                if k.exists(NB):
                    act.wait_ge(x2T_psum, k.at(1, 1))
                    if due(count := k.at(2, 2 * (k.off // 2 * 2 - k.off - 2))):
                        act.wait_ge(uv_psum, count)
                    if due(count := k.at(1, k.off // 2 * 2 - k.off - 2)):
                        act.wait_ge(logit_psum, count)
                    g, b = k.off // 2 % 2, k.off % 2 * P
                    act.copy(x2T[:, g, :, b:b + P], bank_x[:, 0:D].rearrange("p (t n) -> p t n", t=2))\
                        .then_inc(x2T_out, 1)

            run(act, slot)

        @block.vector
        def _(dve):
            dve.memset(val1[:], 0.0).then_inc(const_set, 1)
            dve.memset(val2[:], 0.0).then_inc(const_set, 1)
            dve.memset(mhalf[:], -0.5).then_inc(const_set, 1)
            dve.wait_ge(const_set, 3)
            dve.memset(val1[:, :, :, HD:HD + 1], 1.0).then_inc(const_set, 1)
            dve.memset(val2[:, :, :, HD:HD + 1], 1.0).then_inc(const_set, 1)
            dve.wait_ge(const_set, 5)
            dve.wait_ge(consts_in, 16 * 17)

            def maxima(i, k):
                for u in range(UNITS):
                    dve.wait_ge(scores[i], k.at(UNITS, u + 1))
                    if u == 0:
                        if due(count := k.at(1, 0)):
                            dve.wait_ge(max_lo[i], count)
                    dve.tensor_reduce(negmax[i][:, HPU * u:HPU * (u + 1)],
                                      bank_s[u % 2][:].rearrange("p (a n) -> p a n", a=HPU),
                                      AX_X, ALU.max, negate=True).then_inc(maxed[i], 1)
                dve.wait_ge(maxed[i], k.at(UNITS, UNITS))
                if due(count := k.at(1, 0)):
                    dve.wait_ge(maxT_psum[i], count)
                dve.tensor_copy(negmax_hl[i][:, 0, :], negmax[i][:]).then_inc(max_hi[i], 1)
                dve.wait_ge(max_hi[i], k.at(1, 1))
                dve.tensor_tensor(negmax_hl[i][:, 1, :], negmax[i][:], negmax_hl[i][:, 0, :], ALU.subtract)\
                    .then_inc(max_lo[i], 1)

            def normalise(i, k):
                heads = bank_o[:].rearrange("p (h v) -> p h v", h=HEADS)
                dve.wait_ge(tok_psum[i], k.at(1, 1))
                if due(count := k.at(1, 0)):
                    dve.wait_ge(normed[i], count)
                dve.reciprocal(rden[i][:], heads[:, :, HD]).then_inc(recip_done[i], 1)
                dve.wait_ge(recip_done[i], k.at(1, 1))
                if due(count := k.at(1, 0)):
                    dve.wait_ge(attT_psum[i], count)
                dve.tensor_tensor(att[i][:], heads[:, :, 0:HD],
                                  rden[i][:, :, None].broadcast_to([P, HEADS, HD]), ALU.mult)\
                    .then_inc(normed[i], 1)

            def residual(i, k, psum, skip):
                if due(count := k.at(1, 0)):
                    dve.wait_ge(ln_out[i], count)
                dve.tensor_tensor(z[i][:], psum, skip, ALU.add).then_inc(summed[i], 1)
                dve.wait_ge(summed[i], k.at(1, 1))
                dve.bn_stats(stats[i][:], z[i][:]).then_inc(stats_out[i], 1)
                count = in_register(dve, k.at(1, 1))
                dve.wait_ge(const_set, 5)
                dve.wait_ge(stats_out[i], count)
                dve.bn_aggr(meanvar[i][:], stats[i][:]).then_inc(mv_out[i], 1)
                dve.wait_ge(mv_out[i], k.at(1, 1))
                if due(count := k.at(1, 0)):
                    dve.wait_ge(rstd_out[i], count)
                dve.tensor_scalar(vareps[i][:], meanvar[i][:, 1:2], EPS, None, ALU.add)\
                    .then_inc(vareps_out[i], 1)

            def layer_norm(i, k, dst):
                dve.wait_ge(rstd_out[i], k.at(1, 1))
                src = z[i][:] if i else z[i][:].rearrange("p (a t d) -> p t d a", t=2, d=HD)
                dve.tensor_scalar(dst, src, meanvar[i][:, 0:1], rstd[i][:, 0:1], ALU.subtract, ALU.mult)\
                    .then_inc(ln_out[i], 1)

            def gates(k):
                def link(n):
                    dve.wait_ge(gate_step, k.at(GATE_STEPS, n))
                dve.wait_ge(logit_psum, k.at(1, 1))
                dve.tensor_copy(logit[:], bank_l[1][:, 0:E]).then_inc(gate_step, 1)
                count = in_register(dve, k.at(GATE_STEPS, 1))
                dve.wait_ge(const_set, 5)
                dve.wait_ge(gate_step, count)
                dve.max(top8[:], logit[:]).then_inc(gate_step, 1)
                count = in_register(dve, k.at(GATE_STEPS, 2))
                dve.wait_ge(const_set, 5)
                dve.wait_ge(gate_step, count)
                dve.max_index(topi[:], top8[:], logit[:]).then_inc(gate_step, 1)
                link(3)
                dve.tensor_copy(topf[:], topi[:, 0:2]).then_inc(gate_step, 1)
                link(4)
                dve.tensor_scalar(first[:], iota_sb[:], topf[:, 0:1], None, ALU.is_equal).then_inc(gate_step, 1)
                link(5)
                dve.scalar_tensor_tensor(out=chosen[:], in0=iota_sb[:], scalar=topf[:, 1:2], in1=first[:],
                                         op0=ALU.is_equal, op1=ALU.add).then_inc(gate_step, 1)
                if due(count := k.at(1, 0)):
                    dve.wait_ge(gexp_out, count)
                dve.tensor_scalar(below[:], logit[:], top8[:, 0:1], None, ALU.subtract).then_inc(gate_step, 1)
                link(7)
                dve.wait_ge(gexp_out, k.at(1, 1))
                dve.tensor_tensor(gsel[:], gexp[:], chosen[:], ALU.mult).then_inc(gate_step, 1)
                link(8)
                dve.tensor_reduce(gsum[:], gsel[:], AX_X, ALU.add).then_inc(gate_step, 1)
                link(9)
                dve.reciprocal(ginv[:], gsum[:]).then_inc(gate_step, 1)
                link(10)
                dve.tensor_scalar(gate[:], gsel[:], ginv[:, 0:1], 0.5, ALU.mult, ALU.mult).then_inc(gate_step, 1)
                link(11)
                if due(count := k.at(1, 0)):
                    dve.wait_ge(gateT_psum, count)
                dve.tensor_copy(gate_parts[:, 0, :], gate[:]).then_inc(gate_step, 1)
                link(12)
                dve.tensor_tensor(gate_r[:], gate[:], gate_parts[:, 0, :], ALU.subtract)\
                    .then_inc(gate_rest, 1)
                dve.wait_ge(gate_rest, k.at(1, 1))
                dve.tensor_copy(gate_parts[:, 1, :], gate_r[:]).then_inc(gate_step, 1)
                link(13)
                dve.tensor_tensor(gate_parts[:, 2, :], gate_r[:], gate_parts[:, 1, :], ALU.subtract)\
                    .then_inc(gate_step, 1)

            def slot(s):
                even = s.off % 2 == 0
                k = s.behind(A1)
                if k.exists(NB):
                    maxima(0, k)
                k = s.behind(X1T)
                if k.exists(NB):
                    b = k.off % 2 * P
                    dve.wait_ge(part1["x1"], k.at(1, 1))
                    if due(count := k.group_at(1, 0)):
                        dve.wait_ge(part3["x1"], count)
                    dve.tensor_tensor(rest["x1"][:, :, b:b + P], bank_x[:, 0:D].rearrange("p (t n) -> p t n", t=2),
                                      part["x1"][:, 0, :, b:b + P], ALU.subtract).then_inc(rest1["x1"], 1)
                k = s.behind(GATE)
                if k.exists(NB):
                    gates(k)
                k = s.behind(POST2)
                if k.exists(NB):
                    normalise(1, k)
                k = s
                if k.exists(NB):
                    name = "q" if even else "k"
                    dve.wait_ge(qk_head, k.at(1, 1))
                    if due(count := k.group_at(1, 0)):
                        dve.wait_ge(part3[name], count)
                    for t in range(2):
                        n = 2 * (not even) + t
                        op = dve.scalar_tensor_tensor(out=rest[name][:, t, :], in0=bank_l[0][:, t * 2 * P:(t + 1) * 2 * P],
                                                      scalar=bqk_sb[:, n:n + 1], in1=part[name][:, 0, t, :],
                                                      op0=ALU.add, op1=ALU.subtract)
                    op.then_inc(qk_rest, 1)
                    dve.wait_ge(v_psum, k.at(1, 1))
                    if due(count := k.at(UNITS, UNITS * (1 - 4))):
                        dve.wait_ge(pv_done[0], count)
                    dve.tensor_tensor(val1[:, k.off % 4, :, 0:HD], bank_l[1][:, 0:D].rearrange("p (h d) -> p h d", h=HEADS),
                                      bv_sb[:].rearrange("p (h d) -> p h d", h=HEADS), ALU.add).then_inc(v_out, 1)
                k = s.behind(3)
                if not even and k.exists(NB):
                    ring = k.off // 2 % 2
                    dve.wait_ge(part1["ctx"], k.group_at(1, 1))
                    if due(count := k.group_at(1, 0)):
                        dve.wait_ge(part3["ctx"], count)
                    dve.tensor_tensor(rest["ctx"][:], ctxT_sb[:, ring], part["ctx"][:, 0], ALU.subtract)\
                        .then_inc(rest1["ctx"], 1)
                k = s.behind(POST2)
                if k.exists(NB):
                    dve.wait_ge(proj_psum[1], k.at(1, 1))
                    dve.wait_ge(x1b_ready, k.at(1, 1))
                    residual(1, k, bank_l[1][:, 0:D], x1b[:, k.off % 4])
                k = s.behind(A2)
                if k.exists(NB):
                    maxima(1, k)
                k = s.behind(POST2)
                if k.exists(NB):
                    if due(count := k.at(1, 1 - 4)):
                        dve.wait_ge(y_psum, count)
                    if due(count := k.at(1, 1 - 4)):
                        dve.wait_ge(summed[2], count)
                    if due(count := k.at(1, 1 - 4)):
                        dve.wait_ge(x2T_psum, count)
                    layer_norm(1, k, x2[:, k.off % 4])
                k = s.behind(A1)
                if k.exists(NB):
                    normalise(0, k)
                k = s.behind(FUP)
                if k.exists(NB):
                    ring, half = k.off // 2 % 2, k.off % 2
                    for f in range(2):
                        dve.wait_ge(tanh_out, k.at(2, f + 1))
                        if due(count := k.at(2, f - 1)):
                            dve.wait_ge(prod_out, count)
                        dve.scalar_tensor_tensor(out=silu[:, f, :], in0=th[:, f, :], scalar=1.0, in1=bank_l[f][:, 0:2 * P],
                                                 op0=ALU.add, op1=ALU.mult).then_inc(silu_out, 1)
                    for f in range(2):
                        dve.wait_ge(silu_out, k.at(2, f + 1))
                        if due(count := k.at(2, f - 1)):
                            dve.wait_ge(hid_out, count)
                        dve.tensor_tensor(prod[:, f, :], silu[:, f, :], bank_l[f][:, 2 * P:4 * P], ALU.mult)\
                            .then_inc(prod_out, 1)
                    dve.wait_ge(g_psum, k.at(1, 1))
                    if half == 0:
                        if due(count := k.at(1, 2 - 4)):
                            dve.wait_ge(y_psum, count)
                    for f in range(2):
                        dve.wait_ge(prod_out, k.at(2, f + 1))
                        dve.tensor_tensor(hid[:, ring, 2 * half + f, :], prod[:, f, :],
                                          bank_o[:, f * 2 * P:(f + 1) * 2 * P], ALU.mult).then_inc(hid_out, 1)
                k = s.behind(A1)
                if k.exists(NB):
                    dve.wait_ge(proj_psum[0], k.at(1, 1))
                    dve.wait_ge(xb_ready, k.group_at(1, 1))
                    residual(0, k, bank_l[1][:, 0:D], xtok_sb[:, k.off // 2 % 2, k.off % 2])
                k = s.behind(Y)
                if k.exists(NB):
                    dve.wait_ge(y_psum, k.at(1, 1))
                    residual(2, k, bank_l[0][:, 0:D], x2[:, k.off % 4])
                k = s.behind(A1)
                if k.exists(NB):
                    if due(count := k.at(1, 1 - 4)):
                        dve.wait_ge(x1T_psum, count)
                    if due(count := k.at(1, 1 - 4)):
                        dve.wait_ge(x1b_ready, count)
                    layer_norm(0, k, x1[:, k.off % 4].rearrange("p (t d a) -> p t d a", t=2, d=HD))
                k = s.behind(Y)
                if k.exists(NB):
                    if due(count := k.behind(2).at(8, 16 - 8 * (k.off % 2)) if k.behind(2).exists(NB) else 0):
                        dve.wait_ge(out_written[k.off % 2], count)
                    layer_norm(2, k, y_sb[:, k.off % 2])

            run(dve, slot)

        @block.gpsimd
        def _(pool):
            pool.wait_ge(consts_in, 16 * 17)
            pool.wait_ge(const_set, 5)

            def masking(i, k):
                for u in range(UNITS):
                    count = in_register(pool, k.at(UNITS, u + 1))
                    pool.wait_ge(const_set, 5)
                    pool.wait_ge(exped[i], count)
                    if i == 0:
                        pr = probs[:, u]
                        pool.affine_select(out=pr, in_=pr, compare_op=ALU.is_ge, fill=0.0, base=0,
                                           pattern=[[0, HPU], [-1, P]], channel_multiplier=1).then_inc(masked[0], 1)
                    else:
                        W = P // 2
                        hi, lo = probs[:, u, :, W:P], probs[:, u, :, 0:W]
                        pool.affine_select(out=hi, in_=hi, compare_op=ALU.is_ge, fill=0.0, base=0,
                                           pattern=[[0, HPU], [-1, W]], channel_multiplier=1)
                        pool.affine_select(out=lo, in_=lo, compare_op=ALU.is_ge, fill=0.0, base=W,
                                           pattern=[[0, HPU], [1, W]], channel_multiplier=-1).then_inc(masked[1], 1)

            def inverse_std(i, k):
                pool.wait_ge(vareps_out[i], k.at(1, 1))
                if due(count := k.at(1, 0)):
                    pool.wait_ge(ln_out[i], count)
                pool.tensor_tensor(rstd[i][:], vareps[i][:], mhalf[:], ALU.pow).then_inc(rstd_out[i], 1)

            def split(name, k):
                if due(count := k.behind(2).use_at(16 * TERMS, 16 * TERMS) if k.behind(2).exists(NB) else 0):
                    count = in_register(pool, count)
                    pool.wait_ge(const_set, 5)
                    pool.wait_ge(stacked[name][(k.off // 2 - 1) % 2], count)
                pool.tensor_scalar(part[name][:, 1], rest[name][:], 1.0, 0.0, ALU.mult, ALU.add)\
                    .then_inc(part2[name], 1)
                pool.wait_ge(part2[name], k.group_at(1, 1))
                pool.tensor_tensor(part[name][:, 2], rest[name][:], part[name][:, 1], ALU.subtract)\
                    .then_inc(part3[name], 1)

            def slot(s):
                even = s.off % 2 == 0
                k = s.behind(X1T)
                if k.exists(NB) and k.off % 2 == 1:
                    count = in_register(pool, k.at(1, 1))
                    pool.wait_ge(const_set, 5)
                    pool.wait_ge(rest1["x1"], count)
                    split("x1", k)
                k = s
                if k.exists(NB):
                    count = in_register(pool, k.at(1, 1))
                    pool.wait_ge(const_set, 5)
                    pool.wait_ge(qk_rest, count)
                    split("q" if even else "k", k)
                k = s.behind(3)
                if not even and k.exists(NB):
                    ring = k.off // 2 % 2
                    pool.wait_ge(xtok_in[ring], k.use_at(16, 16))
                    for b in range(2):
                        op = pool.tensor_tensor(xtok_sb[:, ring, b], xtok_sb[:, ring, b], bout_sb[:], ALU.add)
                    op.then_inc(xb_ready, 1)
                k = s.behind(3)
                if not even and k.exists(NB):
                    count = in_register(pool, k.group_at(1, 1))
                    pool.wait_ge(const_set, 5)
                    pool.wait_ge(rest1["ctx"], count)
                    split("ctx", k)
                k = s.behind(4)
                if k.exists(NB):
                    ring = k.off // 2 % 2
                    count = in_register(pool, k.use_at(16, 16))
                    pool.wait_ge(const_set, 5)
                    pool.wait_ge(ctxtok_in[ring], count)
                    if due(count := k.at(UNITS, UNITS * (1 - 4))):
                        count = in_register(pool, count)
                        pool.wait_ge(const_set, 5)
                        pool.wait_ge(pv_done[1], count)
                    pool.tensor_scalar(val2[:, k.off % 4, :, 0:HD],
                                       ctxtok_sb[:, ring, k.off % 2].rearrange("p (h d) -> p h d", h=HEADS),
                                       1.0, 0.0, ALU.mult, ALU.add).then_inc(val2_ready, 1)
                k = s.behind(A1)
                if k.exists(NB):
                    masking(0, k)
                k = s.behind(POST2)
                if k.exists(NB):
                    inverse_std(1, k)
                k = s.behind(A2)
                if k.exists(NB):
                    masking(1, k)
                k = s.behind(A1)
                if k.exists(NB):
                    inverse_std(0, k)
                k = s.behind(Y)
                if k.exists(NB):
                    inverse_std(2, k)
                k = s.behind(A1)
                if k.exists(NB):
                    pool.wait_ge(ln_out[0], k.at(1, 1))
                    if due(count := k.at(1, 1 - 4)):
                        pool.wait_ge(summed[1], count)
                    pool.tensor_tensor(x1b[:, k.off % 4].rearrange("p (a t d) -> p t d a", t=2, d=HD),
                                       x1[:, k.off % 4].rearrange("p (t d a) -> p t d a", t=2, d=HD),
                                       bproj_sb[:].rearrange("p (a t d) -> p t d a", t=2, d=HD), ALU.add)\
                        .then_inc(x1b_ready, 1)

            run(pool, slot)


def kernel(x, ctx_1024, L0_attn_w_qkv, L0_attn_b_qkv, L0_attn_w_out, L0_attn_b_out, L0_xattn_W_proj,
           L0_xattn_b_proj, L0_ffn_gate_w, L0_ffn_Wu, L0_ffn_Wv, L0_ffn_Wo):
    import ml_dtypes
    import numpy as np
    import concourse.bacc as bacc
    from concourse.bass_utils import run_bass_kernel_spmd

    x, c, wqkv, bqkv, wout, bout, wproj, bproj, gw, wu, wv, wo = (
        np.asarray(a) for a in (x, ctx_1024, L0_attn_w_qkv, L0_attn_b_qkv, L0_attn_w_out, L0_attn_b_out,
                                L0_xattn_W_proj, L0_xattn_b_proj, L0_ffn_gate_w, L0_ffn_Wu, L0_ffn_Wv, L0_ffn_Wo))
    NB, S = x.shape[:2]
    NG = NB // 2
    bf16 = ml_dtypes.bfloat16
    qk_w = wqkv[:, :2 * D].reshape(D, 2, 8, 2, HD).transpose(0, 1, 3, 4, 2).reshape(D, 2 * D)
    i, j = np.arange(P)[:, None], np.arange(P)[None, :]
    allowed = np.stack([j >= i, abs(i - j) <= 64], axis=1)
    rows2, rows3 = np.arange(2 * HEADS), np.arange(3 * E)
    arrays = dict(
        x=x,
        xT=x.reshape(NG, 2, S, KT, P).transpose(0, 4, 3, 1, 2).reshape(NG, P, KT, 2 * S),
        ctx_tok=c,
        ctxT=c.reshape(NG, 2, S, 8, 2, HD).transpose(0, 5, 3, 4, 1, 2).reshape(NG, P, 2, 2 * S),
        w_qkv=np.concatenate([qk_w, wqkv[:, 2 * D:]], axis=1),
        b_qk=bqkv[:2 * D].reshape(2, 8, 2, HD).transpose(3, 1, 0, 2).reshape(P, 4),
        b_v=bqkv[2 * D:], w_out=wout, b_out=bout, w_proj=wproj.T, b_proj=bproj, gate_w=gw,
        w_u=wu.transpose(1, 0, 2).reshape(D, E * R), w_v=wv.transpose(1, 0, 2).reshape(D, E * R),
        w_o=wo.reshape(E * R, D),
        ident=np.eye(P, dtype=np.float32),
        ident_bf=np.eye(P).astype(bf16),
        masks=np.where(allowed, 0.0, -3e38).astype(bf16),
        head_sel=np.broadcast_to((rows2[:, None] % HEADS == np.arange(HEADS))[:, :, None],
                                 (2 * HEADS, HEADS, P)).astype(bf16),
        expert_sel=(rows3[:, None, None] % E == 2 * np.arange(FT)[:, None] + np.arange(P) // R).astype(bf16),
        iota8=np.arange(E, dtype=np.float32),
    )
    arrays = {n: np.ascontiguousarray(a) for n, a in arrays.items()}
    nc = bacc.Bacc("TRN2", target_bir_lowering=False, num_devices=1)
    args = {n: nc.dram_tensor(f"in_{n}", a.shape, mybir.dt.from_np(a.dtype), kind="ExternalInput").ap()
            for n, a in arrays.items()}
    out = nc.dram_tensor("out", x.shape, F32, kind="ExternalOutput").ap()
    decoder_layer(nc, **args, out=out)
    r = run_bass_kernel_spmd(nc, [{f"in_{n}": a for n, a in arrays.items()}], core_ids=[0])
    return r.results[0]["out"]
```

```python
from contextlib import ExitStack

import concourse.bass as bass
from concourse import mybir

ALU = mybir.AluOpType
ACT = mybir.ActivationFunctionType
F32 = mybir.dt.float32
BF16 = mybir.dt.bfloat16
U32 = mybir.dt.uint32
AX_X = mybir.AxisListType.X

P = 128
D = 256
KT = D // P
HEADS, HD = 16, 16
UNITS = 4
HPU = HEADS // UNITS
VW = 32
E, R = 8, 64
FT = E * R // P
TERMS = 6
KS = TERMS * HD
Q_PARTS = (0, 0, 0, 1, 1, 2)
K_PARTS = (0, 1, 2, 0, 1, 0)
UNROLL = 4
EPS = 1e-5
SCALE = HD ** -0.5

S1, S2 = 3, 6
T1, T2 = 3, 7
POST1, POST2 = 4, 7
GATE = 8
FUP = 9
Y = 11


class Slot:

    def __init__(self, turn, off):
        self.turn, self.off = turn, off

    def behind(self, lag):
        return Slot(self.turn, self.off - lag)

    def at(self, per, more):
        return self.turn * (UNROLL * per) + (self.off * per + more)

    def group_at(self, per, more):
        return self.turn * (UNROLL // 2 * per) + (self.off // 2 * per + more)

    def use_at(self, per, more):
        return self.turn * per + (self.off // 4 * per + more)

    def exists(self, n):
        return not isinstance(self.turn, int) or 0 <= UNROLL * self.turn + self.off < n


def due(count):
    return not isinstance(count, int) or count > 0


def in_register(eng, count):
    return count if isinstance(count, int) else eng.to_reg(count)


def decoder_layer(nc, x, xT, ctx_tok, ctxT, w_qkv, b_qk, b_v, w_out, b_out, w_proj, b_proj,
                  gate_w, w_u, w_v, w_o, ident, ident_bf, masks, expert_sel, iota8, out):
    NB = x.shape[0]
    NG = NB // 2
    LAST = (Y + UNROLL) // UNROLL * UNROLL + UNROLL
    assert NB % UNROLL == 0

    with ExitStack() as ctx:
        def sb(name, shape, dt=F32):
            return ctx.enter_context(nc.sbuf_tensor(name, shape, dt))

        def sem(name):
            return ctx.enter_context(nc.semaphore(name))

        wqkv_sb = sb("wqkv_sb", [P, KT, 3 * D])
        bqk_sb = sb("bqk_sb", [P, 4])
        bv_sb = sb("bv_sb", [P, D])
        wout_sb = sb("wout_sb", [P, KT, D])
        bout_sb = sb("bout_sb", [P, D])
        wproj_sb = sb("wproj_sb", [P, KT, D])
        bproj_sb = sb("bproj_sb", [P, D])
        gatew_sb = sb("gatew_sb", [P, KT, E])
        wu_sb = sb("wu_sb", [P, KT, E * R])
        wv_sb = sb("wv_sb", [P, KT, E * R])
        wo_sb = sb("wo_sb", [P, FT, D])
        ident_f = sb("ident_f", [P, P])
        ident_b = sb("ident_b", [P, P], BF16)
        mask_sb = sb("mask_sb", [P, 2, P], BF16)
        expsel_sb = sb("expsel_sb", [3 * E, FT, P], BF16)
        iota_sb = sb("iota_sb", [P, E])
        mhalf = sb("mhalf", [P, 1])

        xT_sb = sb("xT_sb", [P, 2, KT, 2 * P])
        xtok_sb = sb("xtok_sb", [P, 2, 2, D])
        ctxT_sb = sb("ctxT_sb", [P, 2, KT, 2 * P])
        ctxtok_sb = sb("ctxtok_sb", [P, 2, 2, D])
        part = {n: sb(f"part_{n}", [P, 3, KT, 2 * P], BF16) for n in ("q", "k", "x1", "ctx")}
        rest = {n: sb(f"rest_{n}", [P, KT, 2 * P]) for n in ("q", "k", "x1", "ctx")}
        stack = {n: sb(f"stack_{n}", [KS + 2, 2, HEADS, 2 * P], BF16) for n in ("q", "k", "x1", "ctx")}
        val1 = sb("val1", [P, 4, HEADS, VW])
        val2 = sb("val2", [P, 4, HEADS, VW])
        negmax = [sb(f"negmax{i}", [P, HEADS]) for i in (1, 2)]
        negmax_hl = [sb(f"negmax_hl{i}", [P, 2, HEADS], BF16) for i in (1, 2)]
        negmax_T = [sb(f"negmax_T{i}", [2 * HEADS, P], BF16) for i in (1, 2)]
        probs = sb("probs", [P, UNITS, HPU, P])
        o_sb = [sb(f"o_sb{i}", [P, UNITS, P]) for i in (1, 2)]
        rden = [sb(f"rden{i}", [P, HEADS]) for i in (1, 2)]
        att = [sb(f"att{i}", [P, HEADS, HD]) for i in (1, 2)]
        attT = [sb(f"attT{i}", [P, KT, P]) for i in (1, 2)]
        z = [sb(f"z{i}", [P, D]) for i in (1, 2, 3)]
        stats = [sb(f"stats{i}", [P, 6]) for i in (1, 2, 3)]
        meanvar = [sb(f"meanvar{i}", [P, 2]) for i in (1, 2, 3)]
        vareps = [sb(f"vareps{i}", [P, 1]) for i in (1, 2, 3)]
        rstd = [sb(f"rstd{i}", [P, 1]) for i in (1, 2, 3)]
        x1 = sb("x1", [P, 4, D])
        x1b = sb("x1b", [P, 4, D])
        x2 = sb("x2", [P, 4, D])
        x2T = sb("x2T", [P, 2, KT, 2 * P])
        logit = sb("logit", [P, E])
        top8 = sb("top8", [P, 8])
        topi = sb("topi", [P, 8], U32)
        topf = sb("topf", [P, 2])
        first = sb("first", [P, E])
        chosen = sb("chosen", [P, E])
        below = sb("below", [P, E])
        gexp = sb("gexp", [P, E])
        gsel = sb("gsel", [P, E])
        gsum = sb("gsum", [P, 1])
        ginv = sb("ginv", [P, 1])
        gate = sb("gate", [P, E])
        gate_r = sb("gate_r", [P, E])
        gate_parts = sb("gate_parts", [P, 3, E], BF16)
        gateT = sb("gateT", [3 * E, 2, 2 * P], BF16)
        th = sb("th", [P, 2, 2 * P])
        silu = sb("silu", [P, 2, 2 * P])
        prod = sb("prod", [P, 2, 2 * P])
        hid = sb("hid", [P, 2, FT, 2 * P])
        y_sb = sb("y_sb", [P, 2, D])

        bank_s = [ctx.enter_context(nc.psum_tensor(f"bank_s{i}", [P, 512], F32)) for i in range(2)]
        bank_t = [ctx.enter_context(nc.psum_tensor(f"bank_t{i}", [P, 512], F32)) for i in range(2)]
        bank_o = ctx.enter_context(nc.psum_tensor("bank_o", [P, 512], F32))
        bank_x = ctx.enter_context(nc.psum_tensor("bank_x", [P, 512], F32))
        bank_l = [ctx.enter_context(nc.psum_tensor(f"bank_l{i}", [P, 512], F32)) for i in range(2)]

        consts_in = sem("consts_in")
        const_set = sem("const_set")
        xT_in = [sem(f"xT_in{i}") for i in range(2)]
        xtok_in = [sem(f"xtok_in{i}") for i in range(2)]
        ctxT_in = [sem(f"ctxT_in{i}") for i in range(2)]
        ctxtok_in = [sem(f"ctxtok_in{i}") for i in range(2)]
        stacked = {n: [sem(f"stacked_{n}{i}") for i in range(2)] for n in stack}
        out_written = [sem(f"out_written{i}") for i in range(2)]
        qk_psum = sem("qk_psum")
        v_psum = sem("v_psum")
        qk_head = sem("qk_head")
        qk_rest = sem("qk_rest")
        v_out = sem("v_out")
        part1 = {n: sem(f"part1_{n}") for n in ("ctx", "x1")}
        rest1 = {n: sem(f"rest1_{n}") for n in ("ctx", "x1")}
        part2 = {n: sem(f"part2_{n}") for n in part}
        part3 = {n: sem(f"part3_{n}") for n in part}
        xb_ready = sem("xb_ready")
        val2_ready = sem("val2_ready")
        max_rows = [[sem(f"max_rows{i}{j}") for j in range(2)] for i in (1, 2)]
        scores = [sem(f"scores{i}") for i in (1, 2)]
        maxed = [sem(f"maxed{i}") for i in (1, 2)]
        max_hi = [sem(f"max_hi{i}") for i in (1, 2)]
        max_lo = [sem(f"max_lo{i}") for i in (1, 2)]
        maxT_psum = [sem(f"maxT_psum{i}") for i in (1, 2)]
        maxT_out = [sem(f"maxT_out{i}") for i in (1, 2)]
        scoresT = [sem(f"scoresT{i}") for i in (1, 2)]
        exped = [sem(f"exped{i}") for i in (1, 2)]
        masked = [sem(f"masked{i}") for i in (1, 2)]
        pv_done = [sem(f"pv_done{i}") for i in (1, 2)]
        o_out = [sem(f"o_out{i}") for i in (1, 2)]
        tok_psum = [sem(f"tok_psum{i}") for i in (1, 2)]
        recip_done = [sem(f"recip_done{i}") for i in (1, 2)]
        normed = [sem(f"normed{i}") for i in (1, 2)]
        attT_psum = [sem(f"attT_psum{i}") for i in (1, 2)]
        attT_out = [sem(f"attT_out{i}") for i in (1, 2)]
        proj_psum = [sem(f"proj_psum{i}") for i in (1, 2)]
        summed = [sem(f"summed{i}") for i in (1, 2, 3)]
        stats_out = [sem(f"stats_out{i}") for i in (1, 2, 3)]
        mv_out = [sem(f"mv_out{i}") for i in (1, 2, 3)]
        vareps_out = [sem(f"vareps_out{i}") for i in (1, 2, 3)]
        rstd_out = [sem(f"rstd_out{i}") for i in (1, 2, 3)]
        ln_out = [sem(f"ln_out{i}") for i in (1, 2, 3)]
        x1b_ready = sem("x1b_ready")
        x1T_psum = sem("x1T_psum")
        x2T_psum = sem("x2T_psum")
        x2T_out = sem("x2T_out")
        logit_psum = sem("logit_psum")
        gate_step = sem("gate_step")
        gexp_out = sem("gexp_out")
        gate_rest = sem("gate_rest")
        gateT_psum = sem("gateT_psum")
        gateT_out = sem("gateT_out")
        uv_psum = sem("uv_psum")
        g_psum = sem("g_psum")
        tanh_out = sem("tanh_out")
        silu_out = sem("silu_out")
        prod_out = sem("prod_out")
        hid_out = sem("hid_out")
        y_psum = sem("y_psum")
        GATE_STEPS = 14
        CONSTS = 7
        LOADS = 16

        def other_so_far(i, k, per):
            if i == 0:
                o = k.behind(S2 - S1 + 1)
                return o.at(per, per) if o.exists(NB) else 0
            o = k.behind(S1 - S2)
            return o.at(per, per) if o.exists(NB) else per * NB

        block = ctx.enter_context(nc.Block())

        def run(eng, slot_program):
            for s in range(LAST):
                slot_program(Slot(s // UNROLL, s % UNROLL))
            with eng.Fori(LAST // UNROLL, NB // UNROLL - 1) as turn:
                for j in range(UNROLL):
                    slot_program(Slot(turn, j))
            for s in range(NB - UNROLL, NB + LAST):
                slot_program(Slot(s // UNROLL, s % UNROLL))

        @block.sync
        def _(sp):
            loads = [
                (wqkv_sb[:], w_qkv.rearrange("(k p) n -> p k n", p=P)),
                (bqk_sb[:], b_qk), (bv_sb[:], b_v.partition_broadcast(P)),
                (ident_f[:], ident), (ident_b[:], ident_bf), (iota_sb[:], iota8.partition_broadcast(P)),
                (mask_sb[:], masks), (expsel_sb[:], expert_sel),
                (wout_sb[:], w_out.rearrange("(k p) n -> p k n", p=P)),
                (bout_sb[:], b_out.partition_broadcast(P)),
                (wproj_sb[:], w_proj.rearrange("(k p) n -> p k n", p=P)),
                (bproj_sb[:], b_proj.partition_broadcast(P)),
                (gatew_sb[:], gate_w.rearrange("(k p) n -> p k n", p=P)),
                (wu_sb[:], w_u.rearrange("(k p) n -> p k n", p=P)),
                (wv_sb[:], w_v.rearrange("(k p) n -> p k n", p=P)),
                (wo_sb[:], w_o.rearrange("(k p) n -> p k n", p=P)),
            ]
            assert len(loads) == LOADS

            def load_xT(k):
                if due(count := k.at(1, 2 - 4)):
                    sp.wait_ge(v_psum, count)
                sp.dma_start(xT_sb[:, k.off // 2 % 2], xT[k.group_at(1, 0)])\
                    .then_inc(xT_in[k.off // 2 % 2], 16)

            def stack_up(i, name, k, parts, terms):
                ring = k.off // 2 % 2
                free, pair = k.at(UNITS, UNITS * (2 - 4)), in_register(sp, k.group_at(1, 1))
                if due(free):
                    free = in_register(sp, free)
                    sp.wait_ge(scoresT[i], free)
                sp.wait_ge(part2[name], pair)
                sp.wait_ge(part3[name], pair)
                for c in terms:
                    dst = stack[name][HD * c:HD * c + HD, ring].rearrange("p (a t) n -> p a t n", t=2)
                    sp.dma_start(dst, part[name][:, parts[c]]).then_inc(stacked[name][ring], 16)

            def stack_maxima(i, name, k):
                ring, b = k.off // 2 % 2, k.off % 2 * P
                free, this = k.at(UNITS, UNITS * (1 - 4)), in_register(sp, k.at(1, 1))
                if due(free):
                    free = in_register(sp, free)
                    sp.wait_ge(scoresT[i], free)
                sp.wait_ge(maxT_out[i], this)
                sp.dma_start(stack[name][KS:KS + 2, ring, :, b:b + P], negmax_T[i][:])\
                    .then_inc(max_rows[i][k.off % 2], 16)

            def slot(s):
                even = s.off % 2 == 0
                half = range(TERMS // 2), range(TERMS // 2, TERMS)
                k = s.behind(S2 + 1)
                if k.exists(NB):
                    stack_maxima(1, "x1", k)
                k = s.behind(6)
                if even and k.exists(NB):
                    stack_up(1, "x1", k, Q_PARTS, range(TERMS))
                k = s.behind(5)
                if not even and k.exists(NB):
                    stack_up(1, "ctx", k, K_PARTS, range(TERMS))
                k = s.behind(1)
                if not even and k.exists(NB):
                    stack_up(0, "q", k, Q_PARTS, range(TERMS))
                k = s.behind(2)
                if even and k.exists(NB):
                    stack_up(0, "k", k, K_PARTS, half[0])
                k = s.behind(S1)
                if k.exists(NB):
                    stack_maxima(0, "q", k)
                k = s.behind(2)
                if even and k.exists(NB):
                    stack_up(0, "k", k, K_PARTS, half[1])
                k = s.behind(-1)
                if not even and k.exists(NB):
                    load_xT(k)
                k = s.behind(2)
                if even and k.exists(NB):
                    ring = k.off // 2 % 2
                    if due(count := k.at(1, 2 - 4)):
                        sp.wait_ge(summed[0], count)
                    sp.dma_start(xtok_sb[:, ring], x[bass.ds(k.at(1, 0), 2)].rearrange("b s d -> s b d"))\
                        .then_inc(xtok_in[ring], 16)
                    if due(count := k.group_at(1, 1 - 2)):
                        sp.wait_ge(part1["ctx"], count)
                        sp.wait_ge(rest1["ctx"], count)
                    sp.dma_start(ctxT_sb[:, ring], ctxT[k.group_at(1, 0)]).then_inc(ctxT_in[ring], 16)
                    if due(count := k.at(1, 2 - 4)):
                        sp.wait_ge(val2_ready, count)
                    sp.dma_start(ctxtok_sb[:, ring], ctx_tok[bass.ds(k.at(1, 0), 2)].rearrange("b s d -> s b d"))\
                        .then_inc(ctxtok_in[ring], 16)
                k = s.behind(Y)
                if k.exists(NB):
                    sp.wait_ge(ln_out[2], k.at(1, 1))
                    sp.dma_start(out[k.at(1, 0)], y_sb[:, k.off % 2]).then_inc(out_written[k.off % 2], 16)

            load_xT(Slot(0, 0))
            for dst, src in loads:
                sp.dma_start(dst, src).then_inc(consts_in, 16)
            run(sp, slot)
            for i in range(2):
                sp.wait_ge(out_written[i], 16 * NB // 2)

        @block.tensor
        def _(pe):
            pe.wait_ge(consts_in, 16 * LOADS)
            pe.wait_ge(const_set, CONSTS)

            def scores_of(i, k, u, q, kk):
                ring, b = k.off // 2 % 2, k.off % 2 * P
                if u == 0:
                    if k.off % 2 == 0:
                        pe.wait_ge(stacked[q][ring], k.use_at(16 * TERMS, 16 * TERMS))
                        pe.wait_ge(stacked[kk][ring], k.use_at(16 * TERMS, 16 * TERMS))
                    if due(count := other_so_far(i, k, 1)):
                        pe.wait_ge(maxT_out[1 - i], count)
                if u == 1:
                    if i == 0:
                        if due(count := other_so_far(i, k, UNITS)):
                            pe.wait_ge(maxed[1], count)
                    else:
                        o = k.behind(POST1 - S2)
                        pe.wait_ge(summed[0], o.at(1, 1) if o.exists(NB) else NB)
                if u >= 2:
                    pe.wait_ge(maxed[i], k.at(UNITS, u - 1))
                bank = bank_s[u % 2]
                pe.matmul(bank[:], ident_b[:], mask_sb[:, i, None, :].broadcast_to([P, HPU, P]),
                          start=True, stop=False, skip_group_check=True)
                for a in range(HPU):
                    h = HPU * u + a
                    mm = pe.matmul(bank[:, a * P:(a + 1) * P], stack[q][0:KS, ring, h, b:b + P],
                                   stack[kk][0:KS, ring, h, b:b + P], start=False, stop=(a == HPU - 1),
                                   skip_group_check=True)
                mm.then_inc(scores[i], 1)

            def max_transpose(i, k):
                pe.wait_ge(max_lo[i], k.at(1, 1))
                pe.transpose(bank_s[0].bitcast(BF16)[0:2 * HEADS, 0:P],
                             negmax_hl[i][:].rearrange("p c h -> p (c h)"), ident_b[:])\
                    .then_inc(maxT_psum[i], 1)

            def scores_T(i, k, u, q, kk):
                ring, b = k.off // 2 % 2, k.off % 2 * P
                if u == 0:
                    pe.wait_ge(max_rows[i][k.off % 2], k.at(8, 16 - 8 * (k.off % 2)))
                    if due(count := other_so_far(i, k, UNITS)):
                        pe.wait_ge(exped[1 - i], count)
                if u == 1 and i == 1 and k.behind(1).exists(NB):
                    pe.wait_ge(gate_step, k.behind(1).at(GATE_STEPS, 1))
                if u >= 2:
                    pe.wait_ge(exped[i], k.at(UNITS, u - 1))
                for a in range(HPU):
                    h = HPU * u + a
                    mm = pe.matmul(bank_t[u % 2][:, a * P:(a + 1) * P], stack[kk][:, ring, h, b:b + P],
                                   stack[q][:, ring, h, b:b + P], start=True, stop=True)
                mm.then_inc(scoresT[i], 1)

            def weigh(i, k, u, val):
                if u == 0 and i == 0:
                    pe.wait_ge(v_out, k.at(1, 1))
                    o = k.behind(T2 - T1)
                    if o.exists(NB):
                        pe.wait_ge(normed[1], o.at(1, 1))
                    elif due(count := k.at(1, 0)):
                        pe.wait_ge(normed[0], count)
                if u == 0 and i == 1:
                    pe.wait_ge(val2_ready, k.at(1, 1))
                    o = k.behind(POST1 - T2)
                    pe.wait_ge(normed[0], o.at(1, 1) if o.exists(NB) else NB)
                    if due(count := k.at(1, 0)):
                        pe.wait_ge(normed[1], count)
                pe.wait_ge(masked[i], k.at(UNITS, u + 1))
                for a in range(HPU):
                    mm = pe.matmul(bank_o[VW * a:VW * a + VW, u * P:(u + 1) * P],
                                   val[:, k.off % 4, HPU * u + a, :], probs[:, u, a, :], start=True, stop=True,
                                   tile_position=(0, VW * a))
                mm.then_inc(pv_done[i], 1)

            def tokens(i, k):
                pe.wait_ge(o_out[i], k.at(1, 1))
                for u in range(UNITS):
                    mm = pe.transpose(bank_o[:, u * P:(u + 1) * P], o_sb[i][:, u, :], ident_f[:])
                mm.then_inc(tok_psum[i], 1)

            def att_transpose(i, k):
                pe.wait_ge(normed[i], k.at(1, 1))
                for t in range(KT):
                    mm = pe.transpose(bank_x[:, t * P:(t + 1) * P],
                                      att[i][:].rearrange("p h d -> p (h d)")[:, t * P:(t + 1) * P], ident_f[:])
                mm.then_inc(attT_psum[i], 1)

            def project(i, k, w, bank):
                pe.wait_ge(attT_out[i], k.at(1, 1))
                for t in range(KT):
                    mm = pe.matmul(bank[:, 0:D], attT[i][:, t, :], w[:, t, :], start=(t == 0), stop=(t == KT - 1))
                mm.then_inc(proj_psum[i], 1)

            def project_qk(k, t):
                ring, b = k.off // 2 % 2, k.off % 2
                if t == 0:
                    if b == 0:
                        pe.wait_ge(xT_in[ring], k.use_at(16, 16))
                    o = k.behind(1 + FUP)
                    if o.exists(NB):
                        pe.wait_ge(prod_out, o.at(2, 2))
                    elif due(count := k.at(1, 0)):
                        pe.wait_ge(qk_rest, count)
                for c in range(KT):
                    mm = pe.matmul(bank_l[0][:, t * 2 * P:(t + 1) * 2 * P],
                                   wqkv_sb[:, c, (2 * b + t) * P:(2 * b + t + 1) * P], xT_sb[:, ring, c, :],
                                   start=(c == 0), stop=(c == KT - 1))
                if t == 1:
                    mm.then_inc(qk_psum, 1)

            def project_v(k):
                ring, b = k.off // 2 % 2, k.off % 2
                o = k.behind(1 + POST2)
                if o.exists(NB):
                    pe.wait_ge(summed[1], o.at(1, 1))
                elif due(count := k.at(1, 0)):
                    pe.wait_ge(v_out, count)
                for c in range(KT):
                    mm = pe.matmul(bank_l[1][:, 0:D], xT_sb[:, ring, c, b * P:(b + 1) * P],
                                   wqkv_sb[:, c, 2 * D:3 * D], start=(c == 0), stop=(c == KT - 1))
                mm.then_inc(v_psum, 1)

            def project_first(s, k):
                o = s.behind(S1)
                pe.wait_ge(maxed[0], o.at(UNITS, UNITS) if o.exists(NB) else UNITS * NB)
                o = s.behind(S2 + 1)
                if o.exists(NB):
                    pe.wait_ge(maxed[1], o.at(UNITS, UNITS))
                if due(count := k.at(1, 0)):
                    pe.wait_ge(summed[0], count)
                project(0, k, wout_sb, bank_s[1])

            def project_second(s, k):
                if s.behind(FUP).exists(NB):
                    pe.wait_ge(prod_out, s.behind(FUP).at(2, 1))
                elif s.exists(NB):
                    pe.wait_ge(v_out, s.at(1, 1))
                elif due(count := k.at(1, 0)):
                    pe.wait_ge(summed[1], count)
                project(1, k, wproj_sb, bank_l[1])

            def transpose_x1(s, k):
                pe.wait_ge(ln_out[0], k.at(1, 1))
                if s.behind(POST2).exists(NB):
                    pe.wait_ge(attT_out[1], s.behind(POST2).at(1, 1))
                else:
                    pe.wait_ge(attT_out[0], k.at(1, 1))
                for t in range(KT):
                    mm = pe.transpose(bank_x[:, t * P:(t + 1) * P], x1[:, k.off % 4, t * P:(t + 1) * P], ident_f[:])
                mm.then_inc(x1T_psum, 1)

            def transpose_x2(s, k):
                pe.wait_ge(ln_out[1], k.at(1, 1))
                o = s.behind(1 + FUP)
                if o.exists(NB):
                    pe.wait_ge(hid_out, o.at(2, 2))
                else:
                    o = s.behind(1 + POST1)
                    pe.wait_ge(rest1["x1"], o.at(1, 1) if o.exists(NB) else NB)
                for t in range(KT):
                    mm = pe.transpose(bank_x[:, t * P:(t + 1) * P], x2[:, k.off % 4, t * P:(t + 1) * P], ident_f[:])
                mm.then_inc(x2T_psum, 1)

            def gate_logits(s, k):
                pe.wait_ge(x2T_out, k.at(1, 1))
                o = s.behind(1 + T1)
                pe.wait_ge(exped[0], o.at(UNITS, UNITS) if o.exists(NB) else UNITS * NB)
                if s.behind(1 + T2).exists(NB):
                    pe.wait_ge(exped[1], s.behind(1 + T2).at(UNITS, UNITS))
                g, b = k.off // 2 % 2, k.off % 2 * P
                for t in range(KT):
                    mm = pe.matmul(bank_t[1][:, 0:E], x2T[:, g, t, b:b + P], gatew_sb[:, t, :],
                                   start=(t == 0), stop=(t == KT - 1))
                mm.then_inc(logit_psum, 1)

            def transpose_gates(s, k):
                pe.wait_ge(gate_step, k.at(GATE_STEPS, GATE_STEPS))
                pe.wait_ge(x2T_out, k.at(1, 1))
                o = s.behind(POST1)
                pe.wait_ge(attT_out[0], o.at(1, 1) if o.exists(NB) else NB)
                pe.transpose(bank_x.bitcast(BF16)[0:3 * E, 0:P],
                             gate_parts[:].rearrange("p c e -> p (c e)"), ident_b[:]).then_inc(gateT_psum, 1)

            def spread_gates(s, k):
                half = k.off % 2
                if half == 0:
                    pe.wait_ge(gateT_out, k.at(1, 2))
                o = s.behind(POST2)
                pe.wait_ge(attT_out[1], o.at(1, 1) if o.exists(NB) else NB)
                o = s.behind(POST1)
                pe.wait_ge(rest1["x1"], o.at(1, 1) if o.exists(NB) else NB)
                o = s.behind(GATE)
                pe.wait_ge(gateT_out, o.at(1, 1) if o.exists(NB) else NB)
                if due(count := k.at(2, 0)):
                    pe.wait_ge(hid_out, count)
                for f in range(2):
                    mm = pe.matmul(bank_x[:, f * 2 * P:(f + 1) * 2 * P], expsel_sb[:, 2 * half + f, :],
                                   gateT[:, k.off // 2 % 2, :], start=True, stop=True)
                mm.then_inc(g_psum, 1)

            def expert_in(s, k, f, n):
                if n == 0 and f == 0:
                    if s.exists(NB):
                        pe.wait_ge(v_out, s.at(1, 1))
                    elif s.behind(1 + POST2).exists(NB):
                        pe.wait_ge(summed[1], s.behind(1 + POST2).at(1, 1))
                    else:
                        pe.wait_ge(prod_out, k.at(2, -1))
                    if k.off % 2 == 0:
                        pe.wait_ge(x2T_out, k.at(1, 2))
                if n == 0 and f == 1:
                    if s.behind(Y).exists(NB):
                        pe.wait_ge(summed[2], s.behind(Y).at(1, 1))
                    else:
                        pe.wait_ge(qk_rest, s.at(1, 1) if s.exists(NB) else NB)
                ft = 2 * (k.off % 2) + f
                for c in range(KT):
                    mm = pe.matmul(bank_l[1 - f][:, n * 2 * P:(n + 1) * 2 * P],
                                   (wu_sb, wv_sb)[n][:, c, ft * P:(ft + 1) * P], x2T[:, k.off // 2 % 2, c, :],
                                   start=(c == 0), stop=(c == KT - 1))
                if n == 1:
                    mm.then_inc(uv_psum, 1)

            def expert_out(s, k):
                ring, b = k.off // 2 % 2, k.off % 2
                if b == 0:
                    pe.wait_ge(hid_out, k.at(2, 4))
                if s.exists(NB):
                    pe.wait_ge(qk_rest, s.at(1, 1))
                o = s.behind(1 + FUP)
                pe.wait_ge(prod_out, o.at(2, 2) if o.exists(NB) else 2 * NB)
                if due(count := k.at(1, 0)):
                    pe.wait_ge(summed[2], count)
                for f in range(FT):
                    mm = pe.matmul(bank_l[0][:, 0:D], hid[:, ring, f, b * P:(b + 1) * P], wo_sb[:, f, :],
                                   start=(f == 0), stop=(f == FT - 1))
                mm.then_inc(y_psum, 1)

            def slot(s):
                s1, s2, t1, t2 = s.behind(S1), s.behind(S2), s.behind(T1), s.behind(T2)
                post1, post2, gate, fup, y = (s.behind(n) for n in (POST1, POST2, GATE, FUP, Y))
                if post1.exists(NB):
                    weigh(0, post1, 2, val1)
                if s1.exists(NB):
                    scores_of(0, s1, 0, "q", "k")
                if s1.exists(NB):
                    scores_of(0, s1, 1, "q", "k")
                if post1.exists(NB):
                    weigh(0, post1, 3, val1)
                if s.exists(NB):
                    project_qk(s, 0)
                if post1.exists(NB):
                    tokens(0, post1)
                if s1.exists(NB):
                    scores_of(0, s1, 2, "q", "k")
                if gate.exists(NB):
                    transpose_x2(s, gate)
                if s.exists(NB):
                    project_qk(s, 1)
                if s1.exists(NB):
                    scores_of(0, s1, 3, "q", "k")
                if post1.exists(NB):
                    att_transpose_first(s, post1)
                if gate.exists(NB):
                    gate_logits(s, gate)
                if s.exists(NB):
                    project_v(s)
                if t2.exists(NB):
                    scores_T(1, t2, 0, "x1", "ctx")
                if post1.exists(NB):
                    project_first(s, post1)
                if t2.exists(NB):
                    scores_T(1, t2, 1, "x1", "ctx")
                if s1.exists(NB):
                    max_transpose(0, s1)
                if y.exists(NB):
                    expert_out(s, y)
                if t2.exists(NB):
                    weigh(1, t2, 0, val2)
                    scores_T(1, t2, 2, "x1", "ctx")
                if fup.exists(NB):
                    expert_in(s, fup, 0, 0)
                if t2.exists(NB):
                    weigh(1, t2, 1, val2)
                    scores_T(1, t2, 3, "x1", "ctx")
                if fup.exists(NB):
                    expert_in(s, fup, 0, 1)
                if t2.exists(NB):
                    weigh(1, t2, 2, val2)
                if gate.exists(NB):
                    transpose_gates(s, gate)
                if s2.exists(NB):
                    scores_of(1, s2, 0, "x1", "ctx")
                if t2.exists(NB):
                    weigh(1, t2, 3, val2)
                if fup.exists(NB):
                    expert_in(s, fup, 1, 0)
                if s2.exists(NB):
                    scores_of(1, s2, 1, "x1", "ctx")
                if t1.exists(NB):
                    scores_T(0, t1, 0, "q", "k")
                if post2.exists(NB):
                    tokens(1, post2)
                if fup.exists(NB):
                    expert_in(s, fup, 1, 1)
                if s2.exists(NB):
                    scores_of(1, s2, 2, "x1", "ctx")
                if post2.exists(NB):
                    att_transpose_second(s, post2)
                if t1.exists(NB):
                    scores_T(0, t1, 1, "q", "k")
                if s2.exists(NB):
                    scores_of(1, s2, 3, "x1", "ctx")
                if post1.exists(NB):
                    transpose_x1(s, post1)
                if t1.exists(NB):
                    weigh(0, t1, 0, val1)
                    scores_T(0, t1, 2, "q", "k")
                if post2.exists(NB):
                    project_second(s, post2)
                if t1.exists(NB):
                    weigh(0, t1, 1, val1)
                if s2.exists(NB):
                    max_transpose(1, s2)
                if t1.exists(NB):
                    scores_T(0, t1, 3, "q", "k")
                if fup.exists(NB):
                    spread_gates(s, fup)

            def att_transpose_first(s, k):
                if s.behind(GATE).exists(NB):
                    pe.wait_ge(x2T_out, s.behind(GATE).at(1, 1))
                elif due(count := k.at(1, 0)):
                    pe.wait_ge(rest1["x1"], count)
                att_transpose(0, k)

            def att_transpose_second(s, k):
                if s.behind(GATE).exists(NB):
                    pe.wait_ge(gateT_out, s.behind(GATE).at(1, 1))
                att_transpose(1, k)

            run(pe, slot)

        @block.scalar
        def _(act):
            act.wait_ge(consts_in, 16 * LOADS)

            def exponential(i, k, u):
                act.wait_ge(scoresT[i], k.at(UNITS, u + 1))
                if u == 0:
                    if due(count := other_so_far(i, k, UNITS)):
                        act.wait_ge(pv_done[1 - i], count)
                act.activation(probs[:, u].rearrange("p a n -> p (a n)"), bank_t[u % 2][:],
                               ACT.Exp, scale=SCALE).then_inc(exped[i], 1)

            def sums_out(i, k):
                act.wait_ge(pv_done[i], k.at(UNITS, UNITS))
                if due(count := k.at(1, 0)):
                    act.wait_ge(tok_psum[i], count)
                act.copy(o_sb[i][:].rearrange("p u n -> p (u n)"), bank_o[:]).then_inc(o_out[i], 1)

            def max_out(i, k):
                act.wait_ge(maxT_psum[i], k.at(1, 1))
                if due(count := k.at(1, 0) if i == 0 else k.at(1, 0)):
                    o = k.behind(1)
                    act.wait_ge(max_rows[i][o.off % 2], o.at(8, 16 - 8 * (o.off % 2)))
                act.copy(negmax_T[i][:], bank_s[0].bitcast(BF16)[0:2 * HEADS, 0:P]).then_inc(maxT_out[i], 1)

            def att_out(i, k):
                act.wait_ge(attT_psum[i], k.at(1, 1))
                if due(count := k.at(1, 0)):
                    act.wait_ge(proj_psum[i], count)
                act.copy(attT[i][:].rearrange("p t n -> p (t n)"), bank_x[:, 0:D]).then_inc(attT_out[i], 1)

            def parts_stacked(name, k):
                o = k.behind(2)
                if o.exists(NB):
                    act.wait_ge(stacked[name][o.off // 2 % 2], o.use_at(16 * TERMS, 16 * TERMS))

            def tanh(k, f):
                act.wait_ge(uv_psum, k.at(2, f + 1))
                if due(count := k.at(2, f - 1)):
                    act.wait_ge(silu_out, count)
                act.activation(th[:, f, :], bank_l[1 - f][:, 0:2 * P], ACT.Tanh, scale=0.5).then_inc(tanh_out, 1)

            def slot(s):
                even = s.off % 2 == 0
                s1, s2, t1, t2 = s.behind(S1), s.behind(S2), s.behind(T1), s.behind(T2)
                post1, post2, gate, fup, y = (s.behind(n) for n in (POST1, POST2, GATE, FUP, Y))
                if post1.exists(NB):
                    sums_out(0, post1)
                if gate.exists(NB):
                    k = gate
                    act.wait_ge(x2T_psum, k.at(1, 1))
                    if due(count := k.at(2, 2 * (k.off // 2 * 2 - k.off - 2))):
                        act.wait_ge(uv_psum, count)
                    if due(count := k.at(1, k.off // 2 * 2 - k.off - 2)):
                        act.wait_ge(logit_psum, count)
                    g, b = k.off // 2 % 2, k.off % 2 * P
                    act.copy(x2T[:, g, :, b:b + P], bank_x[:, 0:D].rearrange("p (t n) -> p t n", t=2))\
                        .then_inc(x2T_out, 1)
                if s.exists(NB):
                    k = s
                    name = "q" if even else "k"
                    act.wait_ge(qk_psum, k.at(1, 1))
                    parts_stacked(name, k)
                    for t in range(2):
                        n = 2 * (not even) + t
                        op = act.activation(part[name][:, 0, t, :], bank_l[0][:, t * 2 * P:(t + 1) * 2 * P],
                                            ACT.Identity, bias=bqk_sb[:, n:n + 1])
                    op.then_inc(qk_head, 1)
                if post1.exists(NB):
                    att_out(0, post1)
                for u in range(2):
                    if t2.exists(NB):
                        exponential(1, t2, u)
                k = s.behind(3)
                if not even and k.exists(NB):
                    ring = k.off // 2 % 2
                    act.wait_ge(ctxT_in[ring], k.use_at(16, 16))
                    parts_stacked("ctx", k)
                    act.copy(part["ctx"][:, 0], ctxT_sb[:, ring]).then_inc(part1["ctx"], 1)
                if s1.exists(NB):
                    max_out(0, s1)
                if gate.exists(NB):
                    act.wait_ge(gate_step, gate.at(GATE_STEPS, 7))
                    act.activation(gexp[:], below[:], ACT.Exp).then_inc(gexp_out, 1)
                for u in range(2, UNITS):
                    if t2.exists(NB):
                        exponential(1, t2, u)
                if fup.exists(NB):
                    tanh(fup, 0)
                if gate.exists(NB):
                    k = gate
                    act.wait_ge(gateT_psum, k.at(1, 1))
                    if due(count := k.at(1, k.off // 2 * 2 - k.off - 2)):
                        act.wait_ge(g_psum, count)
                    act.copy(gateT[:, k.off // 2 % 2, k.off % 2 * P:(k.off % 2 + 1) * P],
                             bank_x.bitcast(BF16)[0:3 * E, 0:P]).then_inc(gateT_out, 1)
                if post2.exists(NB):
                    sums_out(1, post2)
                if t1.exists(NB):
                    exponential(0, t1, 0)
                if fup.exists(NB):
                    tanh(fup, 1)
                if post2.exists(NB):
                    att_out(1, post2)
                if t1.exists(NB):
                    exponential(0, t1, 1)
                if post1.exists(NB):
                    k = post1
                    b = k.off % 2 * P
                    act.wait_ge(x1T_psum, k.at(1, 1))
                    parts_stacked("x1", k)
                    act.copy(part["x1"][:, 0, :, b:b + P], bank_x[:, 0:D].rearrange("p (t n) -> p t n", t=2))\
                        .then_inc(part1["x1"], 1)
                if t1.exists(NB):
                    exponential(0, t1, 2)
                if s2.exists(NB):
                    max_out(1, s2)
                if t1.exists(NB):
                    exponential(0, t1, 3)

            run(act, slot)

        @block.vector
        def _(dve):
            dve.memset(val1[:], 0.0).then_inc(const_set, 1)
            dve.memset(val2[:], 0.0).then_inc(const_set, 1)
            dve.memset(mhalf[:], -0.5).then_inc(const_set, 1)
            dve.memset(stack["k"][KS:KS + 2], 1.0).then_inc(const_set, 1)
            dve.memset(stack["ctx"][KS:KS + 2], 1.0).then_inc(const_set, 1)
            dve.wait_ge(const_set, 5)
            dve.memset(val1[:, :, :, HD:HD + 1], 1.0).then_inc(const_set, 1)
            dve.memset(val2[:, :, :, HD:HD + 1], 1.0).then_inc(const_set, 1)
            dve.wait_ge(const_set, CONSTS)
            dve.wait_ge(consts_in, 16 * LOADS)

            def maximum(i, k, u):
                dve.wait_ge(scores[i], k.at(UNITS, u + 1))
                if u == 0 and due(count := k.at(1, 0)):
                    dve.wait_ge(max_lo[i], count)
                dve.tensor_reduce(negmax[i][:, HPU * u:HPU * (u + 1)],
                                  bank_s[u % 2][:].rearrange("p (a n) -> p a n", a=HPU),
                                  AX_X, ALU.max, negate=True).then_inc(maxed[i], 1)

            def split_maxima(i, k):
                dve.wait_ge(maxed[i], k.at(UNITS, UNITS))
                if due(count := k.at(1, 0)):
                    dve.wait_ge(maxT_psum[i], count)
                dve.tensor_copy(negmax_hl[i][:, 0, :], negmax[i][:]).then_inc(max_hi[i], 1)
                dve.wait_ge(max_hi[i], k.at(1, 1))
                dve.tensor_tensor(negmax_hl[i][:, 1, :], negmax[i][:], negmax_hl[i][:, 0, :], ALU.subtract)\
                    .then_inc(max_lo[i], 1)

            def normalise(i, k):
                heads = bank_o[:].rearrange("p (h v) -> p h v", h=HEADS)
                dve.wait_ge(tok_psum[i], k.at(1, 1))
                if due(count := k.at(1, 0)):
                    dve.wait_ge(normed[i], count)
                dve.reciprocal(rden[i][:], heads[:, :, HD]).then_inc(recip_done[i], 1)
                dve.wait_ge(recip_done[i], k.at(1, 1))
                if due(count := k.at(1, 0)):
                    dve.wait_ge(attT_psum[i], count)
                dve.tensor_tensor(att[i][:], heads[:, :, 0:HD],
                                  rden[i][:, :, None].broadcast_to([P, HEADS, HD]), ALU.mult)\
                    .then_inc(normed[i], 1)

            def residual(i, k, psum, skip):
                if due(count := k.at(1, 0)):
                    dve.wait_ge(ln_out[i], count)
                dve.tensor_tensor(z[i][:], psum, skip, ALU.add).then_inc(summed[i], 1)
                dve.wait_ge(summed[i], k.at(1, 1))
                dve.bn_stats(stats[i][:], z[i][:]).then_inc(stats_out[i], 1)
                count = in_register(dve, k.at(1, 1))
                dve.wait_ge(const_set, CONSTS)
                dve.wait_ge(stats_out[i], count)
                dve.bn_aggr(meanvar[i][:], stats[i][:]).then_inc(mv_out[i], 1)
                dve.wait_ge(mv_out[i], k.at(1, 1))
                if due(count := k.at(1, 0)):
                    dve.wait_ge(rstd_out[i], count)
                dve.tensor_scalar(vareps[i][:], meanvar[i][:, 1:2], EPS, None, ALU.add)\
                    .then_inc(vareps_out[i], 1)

            def layer_norm(i, k, dst):
                dve.wait_ge(rstd_out[i], k.at(1, 1))
                src = z[i][:] if i else z[i][:].rearrange("p (a t d) -> p t d a", t=2, d=HD)
                dve.tensor_scalar(dst, src, meanvar[i][:, 0:1], rstd[i][:, 0:1], ALU.subtract, ALU.mult)\
                    .then_inc(ln_out[i], 1)

            def gate_link(k, n):
                dve.wait_ge(gate_step, k.at(GATE_STEPS, n))

            def choose(k):
                dve.wait_ge(logit_psum, k.at(1, 1))
                dve.tensor_copy(logit[:], bank_t[1][:, 0:E]).then_inc(gate_step, 1)
                count = in_register(dve, k.at(GATE_STEPS, 1))
                dve.wait_ge(const_set, CONSTS)
                dve.wait_ge(gate_step, count)
                dve.max(top8[:], logit[:]).then_inc(gate_step, 1)
                count = in_register(dve, k.at(GATE_STEPS, 2))
                dve.wait_ge(const_set, CONSTS)
                dve.wait_ge(gate_step, count)
                dve.max_index(topi[:], top8[:], logit[:]).then_inc(gate_step, 1)
                gate_link(k, 3)
                dve.tensor_copy(topf[:], topi[:, 0:2]).then_inc(gate_step, 1)
                gate_link(k, 4)
                dve.tensor_scalar(first[:], iota_sb[:], topf[:, 0:1], None, ALU.is_equal).then_inc(gate_step, 1)
                gate_link(k, 5)
                dve.scalar_tensor_tensor(out=chosen[:], in0=iota_sb[:], scalar=topf[:, 1:2], in1=first[:],
                                         op0=ALU.is_equal, op1=ALU.add).then_inc(gate_step, 1)
                if due(count := k.at(1, 0)):
                    dve.wait_ge(gexp_out, count)
                dve.tensor_scalar(below[:], logit[:], top8[:, 0:1], None, ALU.subtract).then_inc(gate_step, 1)

            def weights(k):
                gate_link(k, 7)
                dve.wait_ge(gexp_out, k.at(1, 1))
                dve.tensor_tensor(gsel[:], gexp[:], chosen[:], ALU.mult).then_inc(gate_step, 1)
                gate_link(k, 8)
                dve.tensor_reduce(gsum[:], gsel[:], AX_X, ALU.add).then_inc(gate_step, 1)
                gate_link(k, 9)
                dve.reciprocal(ginv[:], gsum[:]).then_inc(gate_step, 1)
                gate_link(k, 10)
                dve.tensor_scalar(gate[:], gsel[:], ginv[:, 0:1], 0.5, ALU.mult, ALU.mult).then_inc(gate_step, 1)
                gate_link(k, 11)
                if due(count := k.at(1, 0)):
                    dve.wait_ge(gateT_psum, count)
                dve.tensor_copy(gate_parts[:, 0, :], gate[:]).then_inc(gate_step, 1)
                gate_link(k, 12)
                dve.tensor_tensor(gate_r[:], gate[:], gate_parts[:, 0, :], ALU.subtract)\
                    .then_inc(gate_rest, 1)
                dve.wait_ge(gate_rest, k.at(1, 1))
                dve.tensor_copy(gate_parts[:, 1, :], gate_r[:]).then_inc(gate_step, 1)
                gate_link(k, 13)
                dve.tensor_tensor(gate_parts[:, 2, :], gate_r[:], gate_parts[:, 1, :], ALU.subtract)\
                    .then_inc(gate_step, 1)

            def gated(k, f):
                dve.wait_ge(tanh_out, k.at(2, f + 1))
                if due(count := k.at(2, f - 1)):
                    dve.wait_ge(prod_out, count)
                dve.scalar_tensor_tensor(out=silu[:, f, :], in0=th[:, f, :], scalar=1.0, in1=bank_l[1 - f][:, 0:2 * P],
                                         op0=ALU.add, op1=ALU.mult).then_inc(silu_out, 1)
                dve.wait_ge(silu_out, k.at(2, f + 1))
                if due(count := k.at(2, f - 1)):
                    dve.wait_ge(hid_out, count)
                dve.tensor_tensor(prod[:, f, :], silu[:, f, :], bank_l[1 - f][:, 2 * P:4 * P], ALU.mult)\
                    .then_inc(prod_out, 1)

            def slot(s):
                even = s.off % 2 == 0
                s1, s2, t1, t2 = s.behind(S1), s.behind(S2), s.behind(T1), s.behind(T2)
                post1, post2, gate, fup, y = (s.behind(n) for n in (POST1, POST2, GATE, FUP, Y))
                for u in range(2):
                    if s1.exists(NB):
                        maximum(0, s1, u)
                    if u == 0 and gate.exists(NB):
                        k = gate
                        if due(count := k.at(1, 1 - 4)):
                            dve.wait_ge(summed[2], count)
                            dve.wait_ge(x2T_psum, count)
                        layer_norm(1, k, x2[:, k.off % 4])
                if post1.exists(NB):
                    normalise(0, post1)
                for u in range(2, UNITS):
                    if s1.exists(NB):
                        maximum(0, s1, u)
                if s1.exists(NB):
                    split_maxima(0, s1)
                if s.exists(NB):
                    k = s
                    name = "q" if even else "k"
                    dve.wait_ge(qk_head, k.at(1, 1))
                    if due(count := k.group_at(1, 0)):
                        dve.wait_ge(part3[name], count)
                    for t in range(2):
                        n = 2 * (not even) + t
                        op = dve.scalar_tensor_tensor(out=rest[name][:, t, :], in0=bank_l[0][:, t * 2 * P:(t + 1) * 2 * P],
                                                      scalar=bqk_sb[:, n:n + 1], in1=part[name][:, 0, t, :],
                                                      op0=ALU.add, op1=ALU.subtract)
                    op.then_inc(qk_rest, 1)
                    dve.wait_ge(v_psum, k.at(1, 1))
                    if due(count := k.at(UNITS, UNITS * (1 - 4))):
                        dve.wait_ge(pv_done[0], count)
                    dve.tensor_tensor(val1[:, k.off % 4, :, 0:HD], bank_l[1][:, 0:D].rearrange("p (h d) -> p h d", h=HEADS),
                                      bv_sb[:].rearrange("p (h d) -> p h d", h=HEADS), ALU.add).then_inc(v_out, 1)
                if gate.exists(NB):
                    choose(gate)
                if post1.exists(NB):
                    k = post1
                    dve.wait_ge(proj_psum[0], k.at(1, 1))
                    dve.wait_ge(xb_ready, k.group_at(1, 1))
                    residual(0, k, bank_s[1][:, 0:D], xtok_sb[:, k.off // 2 % 2, k.off % 2])
                if gate.exists(NB):
                    weights(gate)
                if y.exists(NB):
                    k = y
                    dve.wait_ge(y_psum, k.at(1, 1))
                    residual(2, k, bank_l[0][:, 0:D], x2[:, k.off % 4])
                if post1.exists(NB):
                    k = post1
                    if due(count := k.at(1, 1 - 4)):
                        dve.wait_ge(x1T_psum, count)
                        dve.wait_ge(x1b_ready, count)
                    layer_norm(0, k, x1[:, k.off % 4].rearrange("p (t d a) -> p t d a", t=2, d=HD))
                if fup.exists(NB):
                    gated(fup, 0)
                k = s.behind(3)
                if not even and k.exists(NB):
                    dve.wait_ge(part1["ctx"], k.group_at(1, 1))
                    if due(count := k.group_at(1, 0)):
                        dve.wait_ge(part3["ctx"], count)
                    dve.tensor_tensor(rest["ctx"][:], ctxT_sb[:, k.off // 2 % 2], part["ctx"][:, 0], ALU.subtract)\
                        .then_inc(rest1["ctx"], 1)
                if y.exists(NB):
                    k = y
                    o = k.behind(2)
                    if o.exists(NB):
                        dve.wait_ge(out_written[o.off % 2], o.at(8, 16 - 8 * (o.off % 2)))
                    layer_norm(2, k, y_sb[:, k.off % 2])
                for u in range(2):
                    if s2.exists(NB):
                        maximum(1, s2, u)
                if post2.exists(NB):
                    normalise(1, post2)
                if fup.exists(NB):
                    gated(fup, 1)
                for u in range(2, UNITS):
                    if s2.exists(NB):
                        maximum(1, s2, u)
                if post1.exists(NB):
                    k = post1
                    b = k.off % 2 * P
                    dve.wait_ge(part1["x1"], k.at(1, 1))
                    if due(count := k.group_at(1, 0)):
                        dve.wait_ge(part3["x1"], count)
                    dve.tensor_tensor(rest["x1"][:, :, b:b + P], bank_x[:, 0:D].rearrange("p (t n) -> p t n", t=2),
                                      part["x1"][:, 0, :, b:b + P], ALU.subtract).then_inc(rest1["x1"], 1)
                if s2.exists(NB):
                    split_maxima(1, s2)
                if post2.exists(NB):
                    k = post2
                    dve.wait_ge(proj_psum[1], k.at(1, 1))
                    dve.wait_ge(x1b_ready, k.at(1, 1))
                    residual(1, k, bank_l[1][:, 0:D], x1b[:, k.off % 4])
                if fup.exists(NB):
                    k = fup
                    ring, half = k.off // 2 % 2, k.off % 2
                    dve.wait_ge(g_psum, k.at(1, 1))
                    if half == 0 and due(count := k.at(1, 2 - 4)):
                        dve.wait_ge(y_psum, count)
                    for f in range(2):
                        dve.wait_ge(prod_out, k.at(2, f + 1))
                        dve.tensor_tensor(hid[:, ring, 2 * half + f, :], prod[:, f, :],
                                          bank_x[:, f * 2 * P:(f + 1) * 2 * P], ALU.mult).then_inc(hid_out, 1)

            run(dve, slot)

        @block.gpsimd
        def _(pool):
            pool.wait_ge(consts_in, 16 * LOADS)
            pool.wait_ge(const_set, CONSTS)

            def masking(i, k, u):
                count = in_register(pool, k.at(UNITS, u + 1))
                pool.wait_ge(const_set, CONSTS)
                pool.wait_ge(exped[i], count)
                if i == 0:
                    pr = probs[:, u]
                    pool.affine_select(out=pr, in_=pr, compare_op=ALU.is_ge, fill=0.0, base=0,
                                       pattern=[[0, HPU], [-1, P]], channel_multiplier=1).then_inc(masked[0], 1)
                else:
                    W = P // 2
                    hi, lo = probs[:, u, :, W:P], probs[:, u, :, 0:W]
                    pool.affine_select(out=hi, in_=hi, compare_op=ALU.is_ge, fill=0.0, base=0,
                                       pattern=[[0, HPU], [-1, W]], channel_multiplier=1)
                    pool.affine_select(out=lo, in_=lo, compare_op=ALU.is_ge, fill=0.0, base=W,
                                       pattern=[[0, HPU], [1, W]], channel_multiplier=-1).then_inc(masked[1], 1)

            def inverse_std(i, k):
                pool.wait_ge(vareps_out[i], k.at(1, 1))
                if due(count := k.at(1, 0)):
                    pool.wait_ge(ln_out[i], count)
                pool.tensor_tensor(rstd[i][:], vareps[i][:], mhalf[:], ALU.pow).then_inc(rstd_out[i], 1)

            def split(name, k, count, ready):
                count = in_register(pool, count)
                pool.wait_ge(const_set, CONSTS)
                pool.wait_ge(ready, count)
                o = k.behind(2)
                if o.exists(NB):
                    count = in_register(pool, o.use_at(16 * TERMS, 16 * TERMS))
                    pool.wait_ge(const_set, CONSTS)
                    pool.wait_ge(stacked[name][o.off // 2 % 2], count)
                pool.tensor_scalar(part[name][:, 1], rest[name][:], 1.0, 0.0, ALU.mult, ALU.add)\
                    .then_inc(part2[name], 1)
                pool.wait_ge(part2[name], k.group_at(1, 1))
                pool.tensor_tensor(part[name][:, 2], rest[name][:], part[name][:, 1], ALU.subtract)\
                    .then_inc(part3[name], 1)

            def slot(s):
                even = s.off % 2 == 0
                t1, t2 = s.behind(T1), s.behind(T2)
                post1, post2, y = (s.behind(n) for n in (POST1, POST2, Y))
                k = s.behind(POST1 + 1)
                if even and k.exists(NB):
                    split("x1", k, k.at(1, 1), rest1["x1"])
                k = s.behind(1)
                if k.exists(NB):
                    split("k" if even else "q", k, k.at(1, 1), qk_rest)
                k = s.behind(4)
                if even and k.exists(NB):
                    split("ctx", k, k.group_at(1, 1), rest1["ctx"])
                k = s.behind(3)
                if not even and k.exists(NB):
                    ring = k.off // 2 % 2
                    pool.wait_ge(xtok_in[ring], k.use_at(16, 16))
                    for b in range(2):
                        op = pool.tensor_tensor(xtok_sb[:, ring, b], xtok_sb[:, ring, b], bout_sb[:], ALU.add)
                    op.then_inc(xb_ready, 1)
                k = s.behind(4)
                if k.exists(NB):
                    ring = k.off // 2 % 2
                    count = in_register(pool, k.use_at(16, 16))
                    pool.wait_ge(const_set, CONSTS)
                    pool.wait_ge(ctxtok_in[ring], count)
                    if due(count := k.at(UNITS, UNITS * (1 - 4))):
                        count = in_register(pool, count)
                        pool.wait_ge(const_set, CONSTS)
                        pool.wait_ge(pv_done[1], count)
                    pool.tensor_scalar(val2[:, k.off % 4, :, 0:HD],
                                       ctxtok_sb[:, ring, k.off % 2].rearrange("p (h d) -> p h d", h=HEADS),
                                       1.0, 0.0, ALU.mult, ALU.add).then_inc(val2_ready, 1)
                k = s.behind(POST1 + 1)
                if k.exists(NB):
                    pool.wait_ge(ln_out[0], k.at(1, 1))
                    if due(count := k.at(1, 1 - 4)):
                        pool.wait_ge(summed[1], count)
                    pool.tensor_tensor(x1b[:, k.off % 4].rearrange("p (a t d) -> p t d a", t=2, d=HD),
                                       x1[:, k.off % 4].rearrange("p (t d a) -> p t d a", t=2, d=HD),
                                       bproj_sb[:].rearrange("p (a t d) -> p t d a", t=2, d=HD), ALU.add)\
                        .then_inc(x1b_ready, 1)
                for u in range(2):
                    if t2.exists(NB):
                        masking(1, t2, u)
                if post1.exists(NB):
                    inverse_std(0, post1)
                for u in range(2, UNITS):
                    if t2.exists(NB):
                        masking(1, t2, u)
                if y.exists(NB):
                    inverse_std(2, y)
                for u in range(UNITS):
                    if t1.exists(NB):
                        masking(0, t1, u)
                if post2.exists(NB):
                    inverse_std(1, post2)

            run(pool, slot)


def kernel(x, ctx_1024, L0_attn_w_qkv, L0_attn_b_qkv, L0_attn_w_out, L0_attn_b_out, L0_xattn_W_proj,
           L0_xattn_b_proj, L0_ffn_gate_w, L0_ffn_Wu, L0_ffn_Wv, L0_ffn_Wo):
    import ml_dtypes
    import numpy as np
    import concourse.bacc as bacc
    from concourse.bass_utils import run_bass_kernel_spmd

    x, c, wqkv, bqkv, wout, bout, wproj, bproj, gw, wu, wv, wo = (
        np.asarray(a) for a in (x, ctx_1024, L0_attn_w_qkv, L0_attn_b_qkv, L0_attn_w_out, L0_attn_b_out,
                                L0_xattn_W_proj, L0_xattn_b_proj, L0_ffn_gate_w, L0_ffn_Wu, L0_ffn_Wv, L0_ffn_Wo))
    NB, S = x.shape[:2]
    NG = NB // 2
    bf16 = ml_dtypes.bfloat16
    qk_w = wqkv[:, :2 * D].reshape(D, 2, 8, 2, HD).transpose(0, 1, 3, 4, 2).reshape(D, 2 * D)
    i, j = np.arange(P)[:, None], np.arange(P)[None, :]
    allowed = np.stack([j >= i, abs(i - j) <= 64], axis=1)
    rows3 = np.arange(3 * E)
    arrays = dict(
        x=x,
        xT=x.reshape(NG, 2, S, KT, P).transpose(0, 4, 3, 1, 2).reshape(NG, P, KT, 2 * S),
        ctx_tok=c,
        ctxT=c.reshape(NG, 2, S, 8, 2, HD).transpose(0, 5, 3, 4, 1, 2).reshape(NG, P, 2, 2 * S),
        w_qkv=np.concatenate([qk_w, wqkv[:, 2 * D:]], axis=1),
        b_qk=bqkv[:2 * D].reshape(2, 8, 2, HD).transpose(3, 1, 0, 2).reshape(P, 4),
        b_v=bqkv[2 * D:], w_out=wout, b_out=bout, w_proj=wproj.T, b_proj=bproj, gate_w=gw,
        w_u=wu.transpose(1, 0, 2).reshape(D, E * R), w_v=wv.transpose(1, 0, 2).reshape(D, E * R),
        w_o=wo.reshape(E * R, D),
        ident=np.eye(P, dtype=np.float32),
        ident_bf=np.eye(P).astype(bf16),
        masks=np.where(allowed, 0.0, -3e38).astype(bf16),
        expert_sel=(rows3[:, None, None] % E == 2 * np.arange(FT)[:, None] + np.arange(P) // R).astype(bf16),
        iota8=np.arange(E, dtype=np.float32),
    )
    arrays = {n: np.ascontiguousarray(a) for n, a in arrays.items()}
    nc = bacc.Bacc("TRN2", target_bir_lowering=False, num_devices=1)
    args = {n: nc.dram_tensor(f"in_{n}", a.shape, mybir.dt.from_np(a.dtype), kind="ExternalInput").ap()
            for n, a in arrays.items()}
    out = nc.dram_tensor("out", x.shape, F32, kind="ExternalOutput").ap()
    decoder_layer(nc, **args, out=out)
    r = run_bass_kernel_spmd(nc, [{f"in_{n}": a for n, a in arrays.items()}], core_ids=[0])
    return r.results[0]["out"]
```

```python
from contextlib import ExitStack

import concourse.bass as bass
from concourse import mybir

ALU = mybir.AluOpType
ACT = mybir.ActivationFunctionType
F32 = mybir.dt.float32
F32R = mybir.dt.float32r
BF16 = mybir.dt.bfloat16
U32 = mybir.dt.uint32
AX_X = mybir.AxisListType.X

P = 128
D = 256
KT = D // P
HEADS, HD = 16, 16
UNITS = 4
HPU = HEADS // UNITS
VW = 32
E, R = 8, 64
FT = E * R // P
TERMS = 6
KS = TERMS * HD
Q_PARTS = (0, 0, 0, 1, 1, 2)
K_PARTS = (0, 1, 2, 0, 1, 0)
PRODUCTS = tuple((c, wp, xp) for c in range(KT) for wp, xp in ((0, 0), (0, 1), (1, 0)))
UNROLL = 4
EPS = 1e-5
SCALE = HD ** -0.5

S1, S2 = 3, 6
T1, T2 = 3, 7
POST1, POST2 = 4, 7
GATE = 8
FUP = 9
Y = 11


class Slot:

    def __init__(self, turn, off):
        self.turn, self.off = turn, off

    def behind(self, lag):
        return Slot(self.turn, self.off - lag)

    def at(self, per, more):
        return self.turn * (UNROLL * per) + (self.off * per + more)

    def group_at(self, per, more):
        return self.turn * (UNROLL // 2 * per) + (self.off // 2 * per + more)

    def use_at(self, per, more):
        return self.turn * per + (self.off // 4 * per + more)

    def exists(self, n):
        return not isinstance(self.turn, int) or 0 <= UNROLL * self.turn + self.off < n


def due(count):
    return not isinstance(count, int) or count > 0


def in_register(eng, count):
    return count if isinstance(count, int) else eng.to_reg(count)


def decoder_layer(nc, x, xT, ctx_tok, ctxT, w_qkv, b_qk, b_v, w_out, b_out, w_proj, b_proj,
                  gate_w, w_u, w_v, w_o, ident, ident_bf, masks, expert_sel, iota8, out):
    NB = x.shape[0]
    NG = NB // 2
    LAST = (Y + UNROLL) // UNROLL * UNROLL + UNROLL
    assert NB % UNROLL == 0

    with ExitStack() as ctx:
        def sb(name, shape, dt=F32):
            return ctx.enter_context(nc.sbuf_tensor(name, shape, dt))

        def sem(name):
            return ctx.enter_context(nc.semaphore(name))

        wqkv_hl = sb("wqkv_hl", [P, 2, KT, 3 * D], F32R)
        bqk_sb = sb("bqk_sb", [P, 4])
        bv_col = sb("bv_col", [P, KT])
        wout_sb = sb("wout_sb", [P, KT, D])
        bout_sb = sb("bout_sb", [P, D])
        wproj_sb = sb("wproj_sb", [P, KT, D])
        bproj_sb = sb("bproj_sb", [P, D])
        gatew_sb = sb("gatew_sb", [P, KT, E])
        wu_hl = sb("wu_hl", [P, 2, KT, E * R], F32R)
        wv_hl = sb("wv_hl", [P, 2, KT, E * R], F32R)
        wo_sb = sb("wo_sb", [P, FT, D])
        ident_f = sb("ident_f", [P, P])
        ident_b = sb("ident_b", [P, P], BF16)
        mask_sb = sb("mask_sb", [P, 2, P], BF16)
        expsel_sb = sb("expsel_sb", [3 * E, FT, P], BF16)
        iota_sb = sb("iota_sb", [P, E])
        mhalf = sb("mhalf", [P, 1])

        xT_sb = sb("xT_sb", [P, KT, 2 * P])
        xT_hl = sb("xT_hl", [P, 2, 2, KT, 2 * P], F32R)
        xtok_sb = sb("xtok_sb", [P, 2, 2, D])
        ctxT_sb = sb("ctxT_sb", [P, KT, 2 * P])
        ctxtok_sb = sb("ctxtok_sb", [P, 2, 2, D])
        part = {n: sb(f"part_{n}", [P, 3, KT, 2 * P], BF16) for n in ("q", "k", "x1", "ctx")}
        rest = {n: sb(f"rest_{n}", [P, KT, 2 * P]) for n in ("q", "k", "x1")}
        rest["ctx"] = ctxT_sb
        stack = {n: sb(f"stack_{n}", [KS + 2, 2, HEADS, 2 * P], BF16) for n in ("q", "k", "x1", "ctx")}
        val1 = sb("val1", [P, 4, HEADS, VW])
        val2 = sb("val2", [P, 4, HEADS, VW])
        negmax = [sb(f"negmax{i}", [P, HEADS]) for i in (1, 2)]
        negmax_hl = [sb(f"negmax_hl{i}", [P, 2, HEADS], BF16) for i in (1, 2)]
        negmax_T = [sb(f"negmax_T{i}", [2 * HEADS, P], BF16) for i in (1, 2)]
        probs = sb("probs", [P, UNITS, HPU, P])
        o_sb = sb("o_sb", [P, UNITS, P])
        rden = [sb(f"rden{i}", [P, HEADS]) for i in (1, 2)]
        att = [sb(f"att{i}", [P, HEADS, HD]) for i in (1, 2)]
        attT = [sb(f"attT{i}", [P, KT, P]) for i in (1, 2)]
        z = [sb(f"z{i}", [P, D]) for i in (1, 2, 3)]
        stats = [sb(f"stats{i}", [P, 6]) for i in (1, 2, 3)]
        meanvar = [sb(f"meanvar{i}", [P, 2]) for i in (1, 2, 3)]
        vareps = [sb(f"vareps{i}", [P, 1]) for i in (1, 2, 3)]
        rstd = [sb(f"rstd{i}", [P, 1]) for i in (1, 2, 3)]
        x1 = sb("x1", [P, 4, D])
        x2 = sb("x2", [P, 4, D])
        x2T = sb("x2T", [P, KT, P])
        x2T_hl = sb("x2T_hl", [P, 2, 2, KT, 2 * P], F32R)
        logit = sb("logit", [P, E])
        top8 = sb("top8", [P, 8])
        topi = sb("topi", [P, 8], U32)
        topf = sb("topf", [P, 2])
        first = sb("first", [P, E])
        chosen = sb("chosen", [P, E])
        below = sb("below", [P, E])
        gexp = sb("gexp", [P, E])
        gsel = sb("gsel", [P, E])
        gsum = sb("gsum", [P, 1])
        ginv = sb("ginv", [P, 1])
        gate = sb("gate", [P, E])
        gate_r = sb("gate_r", [P, E])
        gate_parts = sb("gate_parts", [P, 3, E], BF16)
        gateT = sb("gateT", [3 * E, 2, 2 * P], BF16)
        uv = sb("uv", [P, 2, 2 * P])
        hid = sb("hid", [P, 2, FT, 2 * P])
        y_sb = sb("y_sb", [P, 2, D])
        wqkv_in = probs[:].rearrange("p u a n -> p (u a n)")[:, 0:KT * 3 * D].rearrange("p (k n) -> p k n", k=KT)
        wu_in, wv_in = hid[:, 0].rearrange("p f n -> p (f n)"), hid[:, 1].rearrange("p f n -> p (f n)")
        wu_in, wv_in = (w.rearrange("p (k n) -> p k n", k=KT) for w in (wu_in, wv_in))

        bank_s = [ctx.enter_context(nc.psum_tensor(f"bank_s{i}", [P, 512], F32)) for i in range(2)]
        bank_t = [ctx.enter_context(nc.psum_tensor(f"bank_t{i}", [P, 512], F32)) for i in range(2)]
        bank_o = ctx.enter_context(nc.psum_tensor("bank_o", [P, 512], F32))
        bank_x = ctx.enter_context(nc.psum_tensor("bank_x", [P, 512], F32))
        bank_l = [ctx.enter_context(nc.psum_tensor(f"bank_l{i}", [P, 512], F32)) for i in range(2)]

        consts_in = sem("consts_in")
        const_set = sem("const_set")
        xT_in = sem("xT_in")
        xtok_in = [sem(f"xtok_in{i}") for i in range(2)]
        xT_upper = sem("xT_upper")
        xT_lower = sem("xT_lower")
        ctxT_in = sem("ctxT_in")
        ctxtok_in = [sem(f"ctxtok_in{i}") for i in range(2)]
        stacked = {n: [sem(f"stacked_{n}{i}") for i in range(2)] for n in stack}
        out_written = [sem(f"out_written{i}") for i in range(2)]
        qk_psum = sem("qk_psum")
        v_psum = sem("v_psum")
        qk_head = sem("qk_head")
        qk_rest = sem("qk_rest")
        v_out = sem("v_out")
        part1 = {n: sem(f"part1_{n}") for n in ("ctx", "x1")}
        rest1 = {n: sem(f"rest1_{n}") for n in ("ctx", "x1")}
        part2 = {n: sem(f"part2_{n}") for n in part}
        part3 = {n: sem(f"part3_{n}") for n in part}
        xb_ready = sem("xb_ready")
        val2_ready = sem("val2_ready")
        max_rows = [[sem(f"max_rows{i}{j}") for j in range(2)] for i in (1, 2)]
        scores = [sem(f"scores{i}") for i in (1, 2)]
        maxed = [sem(f"maxed{i}") for i in (1, 2)]
        max_hi = [sem(f"max_hi{i}") for i in (1, 2)]
        max_lo = [sem(f"max_lo{i}") for i in (1, 2)]
        maxT_psum = [sem(f"maxT_psum{i}") for i in (1, 2)]
        maxT_out = [sem(f"maxT_out{i}") for i in (1, 2)]
        scoresT = [sem(f"scoresT{i}") for i in (1, 2)]
        exped = [sem(f"exped{i}") for i in (1, 2)]
        masked = [sem(f"masked{i}") for i in (1, 2)]
        pv_done = [sem(f"pv_done{i}") for i in (1, 2)]
        o_out = [sem(f"o_out{i}") for i in (1, 2)]
        tok_psum = [sem(f"tok_psum{i}") for i in (1, 2)]
        recip_done = [sem(f"recip_done{i}") for i in (1, 2)]
        normed = [sem(f"normed{i}") for i in (1, 2)]
        attT_psum = [sem(f"attT_psum{i}") for i in (1, 2)]
        attT_out = [sem(f"attT_out{i}") for i in (1, 2)]
        proj_psum = [sem(f"proj_psum{i}") for i in (1, 2)]
        summed = [sem(f"summed{i}") for i in (1, 2, 3)]
        stats_out = [sem(f"stats_out{i}") for i in (1, 2, 3)]
        mv_out = [sem(f"mv_out{i}") for i in (1, 2, 3)]
        vareps_out = [sem(f"vareps_out{i}") for i in (1, 2, 3)]
        rstd_out = [sem(f"rstd_out{i}") for i in (1, 2, 3)]
        ln_out = [sem(f"ln_out{i}") for i in (1, 2, 3)]
        x1b_ready = sem("x1b_ready")
        x1T_psum = sem("x1T_psum")
        x2T_psum = sem("x2T_psum")
        x2T_out = sem("x2T_out")
        x2T_upper = sem("x2T_upper")
        x2T_lower = sem("x2T_lower")
        bias_psum = sem("bias_psum")
        logit_psum = sem("logit_psum")
        gate_step = sem("gate_step")
        gexp_out = sem("gexp_out")
        gate_rest = sem("gate_rest")
        gateT_psum = sem("gateT_psum")
        gateT_out = sem("gateT_out")
        uv_psum = sem("uv_psum")
        g_psum = sem("g_psum")
        tanh_out = sem("tanh_out")
        silu_out = sem("silu_out")
        prod_out = sem("prod_out")
        hid_out = sem("hid_out")
        y_psum = sem("y_psum")
        GATE_STEPS = 14
        CONSTS = 14
        LOADS = 16

        def other_so_far(i, k, per):
            if i == 0:
                o = k.behind(S2 - S1 + 1)
                return o.at(per, per) if o.exists(NB) else 0
            o = k.behind(S1 - S2)
            return o.at(per, per) if o.exists(NB) else per * NB

        block = ctx.enter_context(nc.Block())

        def run(eng, slot_program):
            for s in range(-2, LAST):
                slot_program(Slot(s // UNROLL, s % UNROLL))
            with eng.Fori(LAST // UNROLL, NB // UNROLL - 1) as turn:
                for j in range(UNROLL):
                    slot_program(Slot(turn, j))
            for s in range(NB - UNROLL, NB + LAST):
                slot_program(Slot(s // UNROLL, s % UNROLL))

        @block.sync
        def _(sp):
            loads = [
                (wqkv_in, w_qkv.rearrange("(k p) n -> p k n", p=P)),
                (bqk_sb[:], b_qk), (bv_col[:], b_v),
                (ident_f[:], ident), (ident_b[:], ident_bf), (iota_sb[:], iota8.partition_broadcast(P)),
                (mask_sb[:], masks), (expsel_sb[:], expert_sel),
                (wout_sb[:], w_out.rearrange("(k p) n -> p k n", p=P)),
                (bout_sb[:], b_out.partition_broadcast(P)),
                (wproj_sb[:], w_proj.rearrange("(k p) n -> p k n", p=P)),
                (bproj_sb[:], b_proj.partition_broadcast(P)),
                (gatew_sb[:], gate_w.rearrange("(k p) n -> p k n", p=P)),
                (wu_in, w_u.rearrange("(k p) n -> p k n", p=P)),
                (wv_in, w_v.rearrange("(k p) n -> p k n", p=P)),
                (wo_sb[:], w_o.rearrange("(k p) n -> p k n", p=P)),
            ]
            assert len(loads) == LOADS

            def load_xT(k):
                if due(count := k.group_at(1, 0)):
                    sp.wait_ge(xT_lower, count)
                sp.dma_start(xT_sb[:], xT[k.group_at(1, 0)]).then_inc(xT_in, 16)

            def stack_up(i, name, k, parts, terms):
                ring = k.off // 2 % 2
                free, pair = k.at(UNITS, UNITS * (2 - 4)), in_register(sp, k.group_at(1, 1))
                if due(free):
                    free = in_register(sp, free)
                    sp.wait_ge(scoresT[i], free)
                sp.wait_ge(part2[name], pair)
                sp.wait_ge(part3[name], pair)
                for c in terms:
                    dst = stack[name][HD * c:HD * c + HD, ring].rearrange("p (a t) n -> p a t n", t=2)
                    sp.dma_start(dst, part[name][:, parts[c]]).then_inc(stacked[name][ring], 16)

            def stack_maxima(i, name, k):
                ring, b = k.off // 2 % 2, k.off % 2 * P
                free, this = k.at(UNITS, UNITS * (1 - 4)), in_register(sp, k.at(1, 1))
                if due(free):
                    free = in_register(sp, free)
                    sp.wait_ge(scoresT[i], free)
                sp.wait_ge(maxT_out[i], this)
                sp.dma_start(stack[name][KS:KS + 2, ring, :, b:b + P], negmax_T[i][:])\
                    .then_inc(max_rows[i][k.off % 2], 16)

            def slot(s):
                even = s.off % 2 == 0
                half = range(TERMS // 2), range(TERMS // 2, TERMS)
                k = s.behind(S2 + 1)
                if k.exists(NB):
                    stack_maxima(1, "x1", k)
                k = s.behind(6)
                if even and k.exists(NB):
                    stack_up(1, "x1", k, Q_PARTS, range(TERMS))
                k = s.behind(5)
                if not even and k.exists(NB):
                    stack_up(1, "ctx", k, K_PARTS, range(TERMS))
                k = s.behind(1)
                if not even and k.exists(NB):
                    stack_up(0, "q", k, Q_PARTS, range(TERMS))
                k = s.behind(2)
                if even and k.exists(NB):
                    stack_up(0, "k", k, K_PARTS, half[0])
                k = s.behind(S1)
                if k.exists(NB):
                    stack_maxima(0, "q", k)
                k = s.behind(2)
                if even and k.exists(NB):
                    stack_up(0, "k", k, K_PARTS, half[1])
                k = s.behind(-2)
                if even and k.exists(NB):
                    load_xT(k)
                k = s.behind(2)
                if even and k.exists(NB):
                    ring = k.off // 2 % 2
                    if due(count := k.at(1, 2 - 4)):
                        sp.wait_ge(summed[0], count)
                    sp.dma_start(xtok_sb[:, ring], x[bass.ds(k.at(1, 0), 2)].rearrange("b s d -> s b d"))\
                        .then_inc(xtok_in[ring], 16)
                    if due(count := k.group_at(1, 0)):
                        sp.wait_ge(part3["ctx"], count)
                    sp.dma_start(ctxT_sb[:], ctxT[k.group_at(1, 0)]).then_inc(ctxT_in, 16)
                    if due(count := k.at(1, 2 - 4)):
                        sp.wait_ge(val2_ready, count)
                    sp.dma_start(ctxtok_sb[:, ring], ctx_tok[bass.ds(k.at(1, 0), 2)].rearrange("b s d -> s b d"))\
                        .then_inc(ctxtok_in[ring], 16)
                k = s.behind(Y)
                if k.exists(NB):
                    sp.wait_ge(ln_out[2], k.at(1, 1))
                    sp.dma_start(out[k.at(1, 0)], y_sb[:, k.off % 2]).then_inc(out_written[k.off % 2], 16)

            for dst, src in loads:
                sp.dma_start(dst, src).then_inc(consts_in, 16)
            run(sp, slot)
            for i in range(2):
                sp.wait_ge(out_written[i], 16 * NB // 2)

        @block.tensor
        def _(pe):
            pe.wait_ge(consts_in, 16 * LOADS)
            for t in range(KT):
                mm = pe.matmul(bank_x[:, 0:D], bv_col[:, t:t + 1].broadcast_to([P, P]), wout_sb[:, t, :],
                               start=(t == 0), stop=(t == KT - 1))
            mm.then_inc(bias_psum, 1)
            pe.wait_ge(const_set, CONSTS)

            def scores_of(i, k, u, q, kk):
                ring, b = k.off // 2 % 2, k.off % 2 * P
                if u == 0:
                    if k.off % 2 == 0:
                        pe.wait_ge(stacked[q][ring], k.use_at(16 * TERMS, 16 * TERMS))
                        pe.wait_ge(stacked[kk][ring], k.use_at(16 * TERMS, 16 * TERMS))
                    if due(count := other_so_far(i, k, 1)):
                        pe.wait_ge(maxT_out[1 - i], count)
                if u == 1:
                    if i == 0:
                        if due(count := other_so_far(i, k, UNITS)):
                            pe.wait_ge(maxed[1], count)
                    else:
                        o = k.behind(POST1 - S2)
                        pe.wait_ge(summed[0], o.at(1, 1) if o.exists(NB) else NB)
                if u >= 2:
                    pe.wait_ge(maxed[i], k.at(UNITS, u - 1))
                bank = bank_s[u % 2]
                pe.matmul(bank[:], ident_b[:], mask_sb[:, i, None, :].broadcast_to([P, HPU, P]),
                          start=True, stop=False, skip_group_check=True)
                for a in range(HPU):
                    h = HPU * u + a
                    mm = pe.matmul(bank[:, a * P:(a + 1) * P], stack[q][0:KS, ring, h, b:b + P],
                                   stack[kk][0:KS, ring, h, b:b + P], start=False, stop=(a == HPU - 1),
                                   skip_group_check=True)
                mm.then_inc(scores[i], 1)

            def max_transpose(i, k):
                pe.wait_ge(max_lo[i], k.at(1, 1))
                pe.transpose(bank_s[0].bitcast(BF16)[0:2 * HEADS, 0:P],
                             negmax_hl[i][:].rearrange("p c h -> p (c h)"), ident_b[:])\
                    .then_inc(maxT_psum[i], 1)

            def scores_T(i, k, u, q, kk):
                ring, b = k.off // 2 % 2, k.off % 2 * P
                if u == 0:
                    pe.wait_ge(max_rows[i][k.off % 2], k.at(8, 16 - 8 * (k.off % 2)))
                if u == 1 and i == 1 and k.behind(1).exists(NB):
                    pe.wait_ge(gate_step, k.behind(1).at(GATE_STEPS, 1))
                if u >= 2:
                    pe.wait_ge(exped[i], k.at(UNITS, u - 1))
                for a in range(HPU):
                    h = HPU * u + a
                    mm = pe.matmul(bank_t[u % 2][:, a * P:(a + 1) * P], stack[kk][:, ring, h, b:b + P],
                                   stack[q][:, ring, h, b:b + P], start=True, stop=True)
                mm.then_inc(scoresT[i], 1)

            def weigh(i, k, u, val):
                if u == 0 and i == 0:
                    pe.wait_ge(v_out, k.at(1, 1))
                if u == 0 and i == 1:
                    pe.wait_ge(val2_ready, k.at(1, 1))
                pe.wait_ge(masked[i], k.at(UNITS, u + 1))
                for a in range(HPU):
                    mm = pe.matmul(bank_o[VW * a:VW * a + VW, u * P:(u + 1) * P],
                                   val[:, k.off % 4, HPU * u + a, :], probs[:, u, a, :], start=True, stop=True,
                                   tile_position=(0, VW * a))
                mm.then_inc(pv_done[i], 1)

            def tokens(i, k):
                pe.wait_ge(o_out[i], k.at(1, 1))
                for u in range(UNITS):
                    mm = pe.transpose(bank_o[:, u * P:(u + 1) * P], o_sb[:, u, :], ident_f[:])
                mm.then_inc(tok_psum[i], 1)

            def att_transpose(i, k):
                pe.wait_ge(normed[i], k.at(1, 1))
                for t in range(KT):
                    mm = pe.transpose(bank_x[:, t * P:(t + 1) * P],
                                      att[i][:].rearrange("p h d -> p (h d)")[:, t * P:(t + 1) * P], ident_f[:])
                mm.then_inc(attT_psum[i], 1)

            def project(i, k, w, bank):
                pe.wait_ge(attT_out[i], k.at(1, 1))
                for t in range(KT):
                    mm = pe.matmul(bank[:, 0:D], attT[i][:, t, :], w[:, t, :], start=(t == 0), stop=(t == KT - 1))
                mm.then_inc(proj_psum[i], 1)

            def project_qk(k, t):
                ring, b = k.off // 2 % 2, k.off % 2
                if t == 0:
                    if b == 0:
                        pe.wait_ge(xT_lower, k.group_at(1, 1))
                    o = k.behind(1 + FUP)
                    if o.exists(NB):
                        pe.wait_ge(prod_out, o.at(2, 2))
                    elif due(count := k.at(1, 0)):
                        pe.wait_ge(qk_rest, count)
                for n, (c, wp, xp) in enumerate(PRODUCTS):
                    mm = pe.matmul(bank_l[0][:, t * 2 * P:(t + 1) * 2 * P],
                                   wqkv_hl[:, wp, c, (2 * b + t) * P:(2 * b + t + 1) * P], xT_hl[:, ring, xp, c, :],
                                   start=(n == 0), stop=(n == len(PRODUCTS) - 1))
                if t == 1:
                    mm.then_inc(qk_psum, 1)

            def project_v(k):
                ring, b = k.off // 2 % 2, k.off % 2
                o = k.behind(1 + POST2)
                if o.exists(NB):
                    pe.wait_ge(summed[1], o.at(1, 1))
                elif due(count := k.at(1, 0)):
                    pe.wait_ge(v_out, count)
                for n, (c, wp, xp) in enumerate(PRODUCTS):
                    mm = pe.matmul(bank_l[1][:, 0:D], xT_hl[:, ring, xp, c, b * P:(b + 1) * P],
                                   wqkv_hl[:, wp, c, 2 * D:3 * D], start=(n == 0), stop=(n == len(PRODUCTS) - 1))
                mm.then_inc(v_psum, 1)

            def project_first(s, k):
                o = s.behind(S1)
                if o.exists(NB):
                    pe.wait_ge(maxed[0], o.at(UNITS, UNITS))
                elif s.behind(S2 + 1).exists(NB):
                    pe.wait_ge(maxed[1], s.behind(S2 + 1).at(UNITS, UNITS))
                if not s.behind(S2 + 1).exists(NB) and due(count := k.at(1, 0)):
                    pe.wait_ge(summed[0], count)
                project(0, k, wout_sb, bank_s[1])

            def project_second(s, k):
                if s.behind(FUP).exists(NB):
                    pe.wait_ge(prod_out, s.behind(FUP).at(2, 1))
                elif s.exists(NB):
                    pe.wait_ge(v_out, s.at(1, 1))
                elif due(count := k.at(1, 0)):
                    pe.wait_ge(summed[1], count)
                project(1, k, wproj_sb, bank_l[1])

            def transpose_x1(s, k):
                pe.wait_ge(ln_out[0], k.at(1, 1))
                if s.behind(POST2).exists(NB):
                    pe.wait_ge(attT_out[1], s.behind(POST2).at(1, 1))
                else:
                    pe.wait_ge(attT_out[0], k.at(1, 1))
                for t in range(KT):
                    mm = pe.transpose(bank_x[:, t * P:(t + 1) * P], x1[:, k.off % 4, t * P:(t + 1) * P], ident_f[:])
                mm.then_inc(x1T_psum, 1)

            def transpose_x2(s, k):
                pe.wait_ge(ln_out[1], k.at(1, 1))
                o = s.behind(1 + FUP)
                if o.exists(NB):
                    pe.wait_ge(hid_out, o.at(2, 2))
                else:
                    o = s.behind(1 + POST1)
                    pe.wait_ge(rest1["x1"], o.at(1, 1) if o.exists(NB) else NB)
                for t in range(KT):
                    mm = pe.transpose(bank_x[:, t * P:(t + 1) * P], x2[:, k.off % 4, t * P:(t + 1) * P], ident_f[:])
                mm.then_inc(x2T_psum, 1)

            def gate_logits(s, k):
                pe.wait_ge(x2T_out, k.at(1, 1))
                for t in range(KT):
                    mm = pe.matmul(bank_t[1][:, 0:E], x2T[:, t, :], gatew_sb[:, t, :],
                                   start=(t == 0), stop=(t == KT - 1))
                mm.then_inc(logit_psum, 1)

            def transpose_gates(s, k):
                pe.wait_ge(gate_step, k.at(GATE_STEPS, GATE_STEPS))
                pe.transpose(bank_x.bitcast(BF16)[0:3 * E, 0:P],
                             gate_parts[:].rearrange("p c e -> p (c e)"), ident_b[:]).then_inc(gateT_psum, 1)

            def spread_gates(s, k):
                half = k.off % 2
                o = s.behind(POST1)
                pe.wait_ge(rest1["x1"], o.at(1, 1) if o.exists(NB) else NB)
                if not s.behind(POST2).exists(NB):
                    pe.wait_ge(attT_out[1], NB)
                    o = s.behind(GATE)
                    pe.wait_ge(gateT_out, o.at(1, 1) if o.exists(NB) else NB)
                if not s.behind(GATE).exists(NB) and due(count := k.at(2, 0)):
                    pe.wait_ge(hid_out, count)
                for f in range(2):
                    mm = pe.matmul(bank_x[:, f * 2 * P:(f + 1) * 2 * P], expsel_sb[:, 2 * half + f, :],
                                   gateT[:, k.off // 2 % 2, :], start=True, stop=True)
                mm.then_inc(g_psum, 1)

            def expert_in(s, k, f, n):
                if n == 0 and f == 0:
                    if s.exists(NB):
                        pe.wait_ge(v_out, s.at(1, 1))
                    elif s.behind(1 + POST2).exists(NB):
                        pe.wait_ge(summed[1], s.behind(1 + POST2).at(1, 1))
                    else:
                        pe.wait_ge(prod_out, k.at(2, -1))
                    if k.off % 2 == 0:
                        pe.wait_ge(x2T_lower, k.at(1, 2))
                if n == 0 and f == 1:
                    if s.behind(Y).exists(NB):
                        pe.wait_ge(summed[2], s.behind(Y).at(1, 1))
                    else:
                        pe.wait_ge(qk_rest, s.at(1, 1) if s.exists(NB) else NB)
                ft = 2 * (k.off % 2) + f
                for m, (c, wp, xp) in enumerate(PRODUCTS):
                    mm = pe.matmul(bank_l[1 - f][:, n * 2 * P:(n + 1) * 2 * P],
                                   (wu_hl, wv_hl)[n][:, wp, c, ft * P:(ft + 1) * P], x2T_hl[:, k.off // 2 % 2, xp, c, :],
                                   start=(m == 0), stop=(m == len(PRODUCTS) - 1))
                if n == 1:
                    mm.then_inc(uv_psum, 1)

            def expert_out(s, k):
                ring, b = k.off // 2 % 2, k.off % 2
                if b == 0 and not s.behind(GATE).exists(NB):
                    pe.wait_ge(hid_out, k.at(2, 4))
                if s.exists(NB):
                    pe.wait_ge(qk_rest, s.at(1, 1))
                else:
                    o = s.behind(1 + FUP)
                    pe.wait_ge(prod_out, o.at(2, 2) if o.exists(NB) else 2 * NB)
                    if due(count := k.at(1, 0)):
                        pe.wait_ge(summed[2], count)
                for f in range(FT):
                    mm = pe.matmul(bank_l[0][:, 0:D], hid[:, ring, f, b * P:(b + 1) * P], wo_sb[:, f, :],
                                   start=(f == 0), stop=(f == FT - 1))
                mm.then_inc(y_psum, 1)

            def slot(s):
                s1, s2, t1, t2 = s.behind(S1), s.behind(S2), s.behind(T1), s.behind(T2)
                post1, post2, gate, fup, y = (s.behind(n) for n in (POST1, POST2, GATE, FUP, Y))
                if post1.exists(NB):
                    weigh(0, post1, 2, val1)
                if s1.exists(NB):
                    scores_of(0, s1, 0, "q", "k")
                if s1.exists(NB):
                    scores_of(0, s1, 1, "q", "k")
                if s.exists(NB):
                    project_qk(s, 0)
                if post1.exists(NB):
                    weigh(0, post1, 3, val1)
                if s.exists(NB):
                    project_qk(s, 1)
                if gate.exists(NB):
                    transpose_x2(s, gate)
                if post1.exists(NB):
                    tokens(0, post1)
                for u in range(2, UNITS):
                    if s1.exists(NB):
                        scores_of(0, s1, u, "q", "k")
                if gate.exists(NB):
                    gate_logits(s, gate)
                if post1.exists(NB):
                    att_transpose_first(s, post1)
                if s.exists(NB):
                    project_v(s)
                if t2.exists(NB):
                    scores_T(1, t2, 0, "x1", "ctx")
                if post1.exists(NB):
                    project_first(s, post1)
                if t2.exists(NB):
                    scores_T(1, t2, 1, "x1", "ctx")
                if s1.exists(NB):
                    max_transpose(0, s1)
                if y.exists(NB):
                    expert_out(s, y)
                if t2.exists(NB):
                    weigh(1, t2, 0, val2)
                    scores_T(1, t2, 2, "x1", "ctx")
                if fup.exists(NB):
                    expert_in(s, fup, 0, 0)
                if t2.exists(NB):
                    weigh(1, t2, 1, val2)
                    scores_T(1, t2, 3, "x1", "ctx")
                if fup.exists(NB):
                    expert_in(s, fup, 0, 1)
                if t2.exists(NB):
                    weigh(1, t2, 2, val2)
                if gate.exists(NB):
                    transpose_gates(s, gate)
                if s2.exists(NB):
                    scores_of(1, s2, 0, "x1", "ctx")
                if t2.exists(NB):
                    weigh(1, t2, 3, val2)
                if fup.exists(NB):
                    expert_in(s, fup, 1, 0)
                if s2.exists(NB):
                    scores_of(1, s2, 1, "x1", "ctx")
                if t1.exists(NB):
                    scores_T(0, t1, 0, "q", "k")
                if post2.exists(NB):
                    tokens(1, post2)
                if fup.exists(NB):
                    expert_in(s, fup, 1, 1)
                if s2.exists(NB):
                    scores_of(1, s2, 2, "x1", "ctx")
                if post2.exists(NB):
                    att_transpose_second(s, post2)
                if t1.exists(NB):
                    scores_T(0, t1, 1, "q", "k")
                if s2.exists(NB):
                    scores_of(1, s2, 3, "x1", "ctx")
                if post1.exists(NB):
                    transpose_x1(s, post1)
                if t1.exists(NB):
                    weigh(0, t1, 0, val1)
                    scores_T(0, t1, 2, "q", "k")
                if post2.exists(NB):
                    project_second(s, post2)
                if t1.exists(NB):
                    weigh(0, t1, 1, val1)
                if s2.exists(NB):
                    max_transpose(1, s2)
                if t1.exists(NB):
                    scores_T(0, t1, 3, "q", "k")
                if fup.exists(NB):
                    spread_gates(s, fup)

            def att_transpose_first(s, k):
                if s.behind(GATE).exists(NB):
                    pe.wait_ge(x2T_out, s.behind(GATE).at(1, 1))
                elif due(count := k.at(1, 0)):
                    pe.wait_ge(rest1["x1"], count)
                att_transpose(0, k)

            def att_transpose_second(s, k):
                if s.behind(GATE).exists(NB):
                    pe.wait_ge(gateT_out, s.behind(GATE).at(1, 1))
                att_transpose(1, k)

            run(pe, slot)

        @block.scalar
        def _(act):
            act.wait_ge(consts_in, 16 * LOADS)

            def exponential(i, k, u):
                act.wait_ge(scoresT[i], k.at(UNITS, u + 1))
                if u == 0:
                    if due(count := other_so_far(i, k, UNITS)):
                        act.wait_ge(pv_done[1 - i], count)
                act.activation(probs[:, u].rearrange("p a n -> p (a n)"), bank_t[u % 2][:],
                               ACT.Exp, scale=SCALE).then_inc(exped[i], 1)

            def sums_out(i, k):
                act.wait_ge(pv_done[i], k.at(UNITS, UNITS))
                o = k.behind((POST2 - POST1 + 1, POST1 - POST2)[i])
                if o.exists(NB):
                    act.wait_ge(tok_psum[1 - i], o.at(1, 1))
                elif i == 1:
                    act.wait_ge(tok_psum[0], NB)
                if due(count := k.at(1, 0)):
                    act.wait_ge(tok_psum[i], count)
                act.copy(o_sb[:].rearrange("p u n -> p (u n)"), bank_o[:]).then_inc(o_out[i], 1)

            def max_out(i, k):
                act.wait_ge(maxT_psum[i], k.at(1, 1))
                if due(count := k.at(1, 0) if i == 0 else k.at(1, 0)):
                    o = k.behind(1)
                    act.wait_ge(max_rows[i][o.off % 2], o.at(8, 16 - 8 * (o.off % 2)))
                act.copy(negmax_T[i][:], bank_s[0].bitcast(BF16)[0:2 * HEADS, 0:P]).then_inc(maxT_out[i], 1)

            def att_out(i, k):
                act.wait_ge(attT_psum[i], k.at(1, 1))
                if due(count := k.at(1, 0)):
                    act.wait_ge(proj_psum[i], count)
                act.copy(attT[i][:].rearrange("p t n -> p (t n)"), bank_x[:, 0:D]).then_inc(attT_out[i], 1)

            def parts_stacked(name, k):
                o = k.behind(2)
                if o.exists(NB):
                    act.wait_ge(stacked[name][o.off // 2 % 2], o.use_at(16 * TERMS, 16 * TERMS))

            def tanh(k, f):
                act.wait_ge(uv_psum, k.at(2, f + 1))
                if due(count := k.at(2, f - 1)):
                    act.wait_ge(hid_out, count)
                act.activation(uv[:, f, :], bank_l[1 - f][:, 0:2 * P], ACT.Tanh, scale=0.5).then_inc(tanh_out, 1)

            def slot(s):
                even = s.off % 2 == 0
                s1, s2, t1, t2 = s.behind(S1), s.behind(S2), s.behind(T1), s.behind(T2)
                post1, post2, gate, fup, y = (s.behind(n) for n in (POST1, POST2, GATE, FUP, Y))
                if post1.exists(NB):
                    sums_out(0, post1)
                k = s.behind(-1)
                if not even and k.exists(NB):
                    ring = k.off // 2 % 2
                    act.wait_ge(xT_in, k.group_at(16, 16))
                    if due(count := k.at(1, 2 - 4)):
                        act.wait_ge(v_psum, count)
                    act.copy(xT_hl[:, ring, 0], xT_sb[:]).then_inc(xT_upper, 1)
                if gate.exists(NB):
                    k = gate
                    act.wait_ge(x2T_psum, k.at(1, 1))
                    if due(count := k.at(1, 0)):
                        act.wait_ge(logit_psum, count)
                        act.wait_ge(x2T_lower, count)
                    act.copy(x2T[:], bank_x[:, 0:D].rearrange("p (t n) -> p t n", t=2))\
                        .then_inc(x2T_out, 1)
                if s.exists(NB):
                    k = s
                    name = "q" if even else "k"
                    act.wait_ge(qk_psum, k.at(1, 1))
                    parts_stacked(name, k)
                    for t in range(2):
                        n = 2 * (not even) + t
                        op = act.activation(part[name][:, 0, t, :], bank_l[0][:, t * 2 * P:(t + 1) * 2 * P],
                                            ACT.Identity, bias=bqk_sb[:, n:n + 1])
                    op.then_inc(qk_head, 1)
                if post1.exists(NB):
                    att_out(0, post1)
                if gate.exists(NB):
                    k = gate
                    act.wait_ge(x2T_out, k.at(1, 1))
                    if due(count := k.at(2, 2 * (k.off // 2 * 2 - k.off - 2))):
                        act.wait_ge(uv_psum, count)
                    act.copy(x2T_hl[:, k.off // 2 % 2, 0, :, k.off % 2 * P:(k.off % 2 + 1) * P], x2T[:])\
                        .then_inc(x2T_upper, 1)
                if t2.exists(NB):
                    exponential(1, t2, 0)
                if s.exists(NB):
                    k = s
                    act.wait_ge(v_psum, k.at(1, 1))
                    if due(count := k.at(UNITS, UNITS * (1 - 4))):
                        act.wait_ge(pv_done[0], count)
                    act.copy(val1[:, k.off % 4, :, 0:HD], bank_l[1][:, 0:D].rearrange("p (h d) -> p h d", h=HEADS))\
                        .then_inc(v_out, 1)
                if t2.exists(NB):
                    exponential(1, t2, 1)
                k = s.behind(3)
                if not even and k.exists(NB):
                    act.wait_ge(ctxT_in, k.group_at(16, 16))
                    parts_stacked("ctx", k)
                    act.copy(part["ctx"][:, 0], ctxT_sb[:]).then_inc(part1["ctx"], 1)
                if s1.exists(NB):
                    max_out(0, s1)
                if gate.exists(NB):
                    act.wait_ge(gate_step, gate.at(GATE_STEPS, 6))
                    act.activation(gexp[:], below[:], ACT.Exp).then_inc(gexp_out, 1)
                for u in range(2, UNITS):
                    if t2.exists(NB):
                        exponential(1, t2, u)
                if fup.exists(NB):
                    tanh(fup, 0)
                if gate.exists(NB):
                    k = gate
                    act.wait_ge(gateT_psum, k.at(1, 1))
                    if due(count := k.at(1, k.off // 2 * 2 - k.off - 2)):
                        act.wait_ge(g_psum, count)
                    act.copy(gateT[:, k.off // 2 % 2, k.off % 2 * P:(k.off % 2 + 1) * P],
                             bank_x.bitcast(BF16)[0:3 * E, 0:P]).then_inc(gateT_out, 1)
                if post2.exists(NB):
                    sums_out(1, post2)
                if t1.exists(NB):
                    exponential(0, t1, 0)
                if fup.exists(NB):
                    tanh(fup, 1)
                if post2.exists(NB):
                    att_out(1, post2)
                if t1.exists(NB):
                    exponential(0, t1, 1)
                if post1.exists(NB):
                    k = post1
                    b = k.off % 2 * P
                    act.wait_ge(x1T_psum, k.at(1, 1))
                    parts_stacked("x1", k)
                    act.copy(part["x1"][:, 0, :, b:b + P], bank_x[:, 0:D].rearrange("p (t n) -> p t n", t=2))\
                        .then_inc(part1["x1"], 1)
                if t1.exists(NB):
                    exponential(0, t1, 2)
                if s2.exists(NB):
                    max_out(1, s2)
                if t1.exists(NB):
                    exponential(0, t1, 3)

            run(act, slot)

        @block.vector
        def _(dve):
            dve.memset(val1[:], 0.0).then_inc(const_set, 1)
            dve.memset(val2[:], 0.0).then_inc(const_set, 1)
            dve.memset(mhalf[:], -0.5).then_inc(const_set, 1)
            dve.memset(stack["k"][KS:KS + 2], 1.0).then_inc(const_set, 1)
            dve.memset(stack["ctx"][KS:KS + 2], 1.0).then_inc(const_set, 1)
            dve.wait_ge(const_set, 5)
            dve.memset(val1[:, :, :, HD:HD + 1], 1.0).then_inc(const_set, 1)
            dve.memset(val2[:, :, :, HD:HD + 1], 1.0).then_inc(const_set, 1)
            dve.wait_ge(consts_in, 16 * LOADS)
            for n, (w, hl) in enumerate(((wqkv_in, wqkv_hl), (wu_in, wu_hl), (wv_in, wv_hl))):
                dve.tensor_copy(hl[:, 0], w).then_inc(const_set, 1)
                dve.wait_ge(const_set, 8 + 2 * n)
                dve.tensor_tensor(hl[:, 1], w, hl[:, 0], ALU.subtract).then_inc(const_set, 1)
            dve.wait_ge(bias_psum, 1)
            dve.tensor_tensor(bout_sb[:], bout_sb[:], bank_x[:, 0:D], ALU.add).then_inc(const_set, 1)
            dve.wait_ge(const_set, CONSTS)

            def maximum(i, k, u):
                dve.wait_ge(scores[i], k.at(UNITS, u + 1))
                if u == 0 and due(count := k.at(1, 0)):
                    dve.wait_ge(max_lo[i], count)
                dve.tensor_reduce(negmax[i][:, HPU * u:HPU * (u + 1)],
                                  bank_s[u % 2][:].rearrange("p (a n) -> p a n", a=HPU),
                                  AX_X, ALU.max, negate=True).then_inc(maxed[i], 1)

            def split_maxima(i, k):
                dve.wait_ge(maxed[i], k.at(UNITS, UNITS))
                if due(count := k.at(1, 0)):
                    dve.wait_ge(maxT_psum[i], count)
                dve.tensor_copy(negmax_hl[i][:, 0, :], negmax[i][:]).then_inc(max_hi[i], 1)
                dve.wait_ge(max_hi[i], k.at(1, 1))
                dve.tensor_tensor(negmax_hl[i][:, 1, :], negmax[i][:], negmax_hl[i][:, 0, :], ALU.subtract)\
                    .then_inc(max_lo[i], 1)

            def normalise(i, k):
                heads = bank_o[:].rearrange("p (h v) -> p h v", h=HEADS)
                dve.wait_ge(tok_psum[i], k.at(1, 1))
                if due(count := k.at(1, 0)):
                    dve.wait_ge(normed[i], count)
                dve.reciprocal(rden[i][:], heads[:, :, HD]).then_inc(recip_done[i], 1)
                dve.wait_ge(recip_done[i], k.at(1, 1))
                if due(count := k.at(1, 0)):
                    dve.wait_ge(attT_psum[i], count)
                dve.tensor_tensor(att[i][:], heads[:, :, 0:HD],
                                  rden[i][:, :, None].broadcast_to([P, HEADS, HD]), ALU.mult)\
                    .then_inc(normed[i], 1)

            def residual(i, k, psum, skip):
                if due(count := k.at(1, 0)):
                    dve.wait_ge(ln_out[i], count)
                dst = z[i][:] if i != 1 else z[i][:].rearrange("p (a t d) -> p t d a", t=2, d=HD)
                dve.tensor_tensor(dst, psum, skip, ALU.add).then_inc(summed[i], 1)

            def statistics(i, k):
                dve.wait_ge(summed[i], k.at(1, 1))
                dve.bn_stats(stats[i][:], z[i][:]).then_inc(stats_out[i], 1)

            def mean_variance(i, k):
                count = in_register(dve, k.at(1, 1))
                dve.wait_ge(const_set, CONSTS)
                dve.wait_ge(stats_out[i], count)
                dve.bn_aggr(meanvar[i][:], stats[i][:]).then_inc(mv_out[i], 1)

            def variance_eps(i, k):
                dve.wait_ge(mv_out[i], k.at(1, 1))
                if due(count := k.at(1, 0)):
                    dve.wait_ge(rstd_out[i], count)
                dve.tensor_scalar(vareps[i][:], meanvar[i][:, 1:2], EPS, None, ALU.add)\
                    .then_inc(vareps_out[i], 1)

            def layer_norm(i, k, dst):
                dve.wait_ge(rstd_out[i], k.at(1, 1))
                src = z[i][:] if i else z[i][:].rearrange("p (a t d) -> p t d a", t=2, d=HD)
                dve.tensor_scalar(dst, src, meanvar[i][:, 0:1], rstd[i][:, 0:1], ALU.subtract, ALU.mult)\
                    .then_inc(ln_out[i], 1)

            def gate_step_1(k):
                dve.wait_ge(logit_psum, k.at(1, 1))
                dve.tensor_copy(logit[:], bank_t[1][:, 0:E]).then_inc(gate_step, 1)

            def gate_step_2(k):
                count = in_register(dve, k.at(GATE_STEPS, 1))
                dve.wait_ge(const_set, CONSTS)
                dve.wait_ge(gate_step, count)
                dve.max(top8[:], logit[:]).then_inc(gate_step, 1)

            def gate_step_3(k):
                count = in_register(dve, k.at(GATE_STEPS, 2))
                dve.wait_ge(const_set, CONSTS)
                dve.wait_ge(gate_step, count)
                dve.max_index(topi[:], top8[:], logit[:]).then_inc(gate_step, 1)

            def gate_step_4(k):
                dve.wait_ge(gate_step, k.at(GATE_STEPS, 3))
                dve.tensor_copy(topf[:], topi[:, 0:2]).then_inc(gate_step, 1)

            def gate_step_5(k):
                dve.wait_ge(gate_step, k.at(GATE_STEPS, 4))
                dve.tensor_scalar(first[:], iota_sb[:], topf[:, 0:1], None, ALU.is_equal).then_inc(gate_step, 1)

            def gate_step_6(k):
                if due(count := k.at(1, 0)):
                    dve.wait_ge(gexp_out, count)
                dve.tensor_scalar(below[:], logit[:], top8[:, 0:1], None, ALU.subtract).then_inc(gate_step, 1)

            def gate_step_7(k):
                dve.wait_ge(gate_step, k.at(GATE_STEPS, 5))
                dve.scalar_tensor_tensor(out=chosen[:], in0=iota_sb[:], scalar=topf[:, 1:2], in1=first[:],
                                         op0=ALU.is_equal, op1=ALU.add).then_inc(gate_step, 1)

            def gate_step_8(k):
                dve.wait_ge(gate_step, k.at(GATE_STEPS, 7))
                dve.wait_ge(gexp_out, k.at(1, 1))
                dve.tensor_tensor(gsel[:], gexp[:], chosen[:], ALU.mult).then_inc(gate_step, 1)

            def gate_step_9(k):
                dve.wait_ge(gate_step, k.at(GATE_STEPS, 8))
                dve.tensor_reduce(gsum[:], gsel[:], AX_X, ALU.add).then_inc(gate_step, 1)

            def gate_step_10(k):
                dve.wait_ge(gate_step, k.at(GATE_STEPS, 9))
                dve.reciprocal(ginv[:], gsum[:]).then_inc(gate_step, 1)

            def gate_step_11(k):
                dve.wait_ge(gate_step, k.at(GATE_STEPS, 10))
                dve.tensor_scalar(gate[:], gsel[:], ginv[:, 0:1], 0.5, ALU.mult, ALU.mult).then_inc(gate_step, 1)

            def gate_step_12(k):
                dve.wait_ge(gate_step, k.at(GATE_STEPS, 11))
                if due(count := k.at(1, 0)):
                    dve.wait_ge(gateT_psum, count)
                dve.tensor_copy(gate_parts[:, 0, :], gate[:]).then_inc(gate_step, 1)

            def gate_remainder(k):
                dve.wait_ge(gate_step, k.at(GATE_STEPS, 12))
                dve.tensor_tensor(gate_r[:], gate[:], gate_parts[:, 0, :], ALU.subtract)\
                    .then_inc(gate_rest, 1)

            def gate_step_13(k):
                dve.wait_ge(gate_rest, k.at(1, 1))
                dve.tensor_copy(gate_parts[:, 1, :], gate_r[:]).then_inc(gate_step, 1)

            def gate_step_14(k):
                dve.wait_ge(gate_step, k.at(GATE_STEPS, 13))
                dve.tensor_tensor(gate_parts[:, 2, :], gate_r[:], gate_parts[:, 1, :], ALU.subtract)\
                    .then_inc(gate_step, 1)

            def q_or_k_rest(k, t):
                b = k.off % 2
                name = "qk"[b]
                if t == 0:
                    dve.wait_ge(qk_head, k.at(1, 1))
                    if due(count := k.group_at(1, 0)):
                        dve.wait_ge(part3[name], count)
                n = 2 * b + t
                op = dve.scalar_tensor_tensor(out=rest[name][:, t, :], in0=bank_l[0][:, t * 2 * P:(t + 1) * 2 * P],
                                              scalar=bqk_sb[:, n:n + 1], in1=part[name][:, 0, t, :],
                                              op0=ALU.add, op1=ALU.subtract)
                if t == 1:
                    op.then_inc(qk_rest, 1)

            def gated(k, f):
                dve.wait_ge(tanh_out, k.at(2, f + 1))
                dve.scalar_tensor_tensor(out=uv[:, f, :], in0=uv[:, f, :], scalar=1.0, in1=bank_l[1 - f][:, 0:2 * P],
                                         op0=ALU.add, op1=ALU.mult).then_inc(silu_out, 1)
                dve.wait_ge(silu_out, k.at(2, f + 1))
                dve.tensor_tensor(uv[:, f, :], uv[:, f, :], bank_l[1 - f][:, 2 * P:4 * P], ALU.mult)\
                    .then_inc(prod_out, 1)

            def slot(s):
                even = s.off % 2 == 0
                s1, s2, t1, t2 = s.behind(S1), s.behind(S2), s.behind(T1), s.behind(T2)
                post1, post2, gate, fup, y = (s.behind(n) for n in (POST1, POST2, GATE, FUP, Y))
                for u in range(2):
                    if s1.exists(NB):
                        maximum(0, s1, u)
                    if u == 0 and gate.exists(NB):
                        k = gate
                        if due(count := k.at(1, 1 - 4)):
                            dve.wait_ge(summed[2], count)
                            dve.wait_ge(x2T_psum, count)
                        layer_norm(1, k, x2[:, k.off % 4])
                if post1.exists(NB):
                    normalise(0, post1)
                for u in range(2, UNITS):
                    if s1.exists(NB):
                        maximum(0, s1, u)
                if s1.exists(NB):
                    split_maxima(0, s1)
                if gate.exists(NB):
                    gate_step_1(gate)
                if s.exists(NB):
                    q_or_k_rest(s, 0)
                if gate.exists(NB):
                    gate_step_2(gate)
                if s.exists(NB):
                    q_or_k_rest(s, 1)
                if gate.exists(NB):
                    gate_step_3(gate)
                if post1.exists(NB):
                    dve.wait_ge(proj_psum[0], post1.at(1, 1))
                    dve.wait_ge(xb_ready, post1.group_at(1, 1))
                    residual(0, post1, bank_s[1][:, 0:D], xtok_sb[:, post1.off // 2 % 2, post1.off % 2])
                if gate.exists(NB):
                    gate_step_4(gate)
                if post1.exists(NB):
                    statistics(0, post1)
                if gate.exists(NB):
                    gate_step_5(gate)
                    gate_step_6(gate)
                if post1.exists(NB):
                    mean_variance(0, post1)
                if gate.exists(NB):
                    gate_step_7(gate)
                if post1.exists(NB):
                    variance_eps(0, post1)
                if gate.exists(NB):
                    gate_step_8(gate)
                    gate_step_9(gate)
                if y.exists(NB):
                    dve.wait_ge(y_psum, y.at(1, 1))
                    residual(2, y, bank_l[0][:, 0:D], x2[:, y.off % 4])
                if gate.exists(NB):
                    gate_step_10(gate)
                if y.exists(NB):
                    statistics(2, y)
                if gate.exists(NB):
                    gate_step_11(gate)
                if y.exists(NB):
                    mean_variance(2, y)
                if gate.exists(NB):
                    gate_step_12(gate)
                if y.exists(NB):
                    variance_eps(2, y)
                if gate.exists(NB):
                    gate_remainder(gate)
                if post1.exists(NB):
                    k = post1
                    if due(count := k.at(1, 1 - 4)):
                        dve.wait_ge(summed[1], count)
                    layer_norm(0, k, x1[:, k.off % 4].rearrange("p (t d a) -> p t d a", t=2, d=HD))
                if gate.exists(NB):
                    gate_step_13(gate)
                if gate.exists(NB):
                    gate_step_14(gate)
                if fup.exists(NB):
                    gated(fup, 0)
                k = s.behind(3)
                if not even and k.exists(NB):
                    dve.wait_ge(part1["ctx"], k.group_at(1, 1))
                    dve.tensor_tensor(ctxT_sb[:], ctxT_sb[:], part["ctx"][:, 0], ALU.subtract)\
                        .then_inc(rest1["ctx"], 1)
                if y.exists(NB):
                    k = y
                    o = k.behind(2)
                    if o.exists(NB):
                        dve.wait_ge(out_written[o.off % 2], o.at(8, 16 - 8 * (o.off % 2)))
                    layer_norm(2, k, y_sb[:, k.off % 2])
                for u in range(2):
                    if s2.exists(NB):
                        maximum(1, s2, u)
                if post2.exists(NB):
                    normalise(1, post2)
                if fup.exists(NB):
                    gated(fup, 1)
                for u in range(2, UNITS):
                    if s2.exists(NB):
                        maximum(1, s2, u)
                if post1.exists(NB):
                    k = post1
                    b = k.off % 2 * P
                    dve.wait_ge(part1["x1"], k.at(1, 1))
                    if due(count := k.group_at(1, 0)):
                        dve.wait_ge(part3["x1"], count)
                    dve.tensor_tensor(rest["x1"][:, :, b:b + P], bank_x[:, 0:D].rearrange("p (t n) -> p t n", t=2),
                                      part["x1"][:, 0, :, b:b + P], ALU.subtract).then_inc(rest1["x1"], 1)
                if s2.exists(NB):
                    split_maxima(1, s2)
                if post2.exists(NB):
                    k = post2
                    dve.wait_ge(proj_psum[1], k.at(1, 1))
                    dve.wait_ge(x1b_ready, k.at(1, 1))
                    residual(1, k, bank_l[1][:, 0:D].rearrange("p (a t d) -> p t d a", t=2, d=HD),
                             x1[:, k.off % 4].rearrange("p (t d a) -> p t d a", t=2, d=HD))
                    statistics(1, k)
                    mean_variance(1, k)
                    variance_eps(1, k)
                if fup.exists(NB):
                    k = fup
                    ring, half = k.off // 2 % 2, k.off % 2
                    dve.wait_ge(g_psum, k.at(1, 1))
                    if half == 0 and due(count := k.at(1, 2 - 4)):
                        dve.wait_ge(y_psum, count)
                    for f in range(2):
                        dve.wait_ge(prod_out, k.at(2, f + 1))
                        dve.tensor_tensor(hid[:, ring, 2 * half + f, :], uv[:, f, :],
                                          bank_x[:, f * 2 * P:(f + 1) * 2 * P], ALU.mult).then_inc(hid_out, 1)

            run(dve, slot)

        @block.gpsimd
        def _(pool):
            pool.wait_ge(consts_in, 16 * LOADS)
            pool.wait_ge(const_set, CONSTS)

            def masking(i, k, u):
                count = in_register(pool, k.at(UNITS, u + 1))
                pool.wait_ge(const_set, CONSTS)
                pool.wait_ge(exped[i], count)
                if i == 0:
                    pr = probs[:, u]
                    pool.affine_select(out=pr, in_=pr, compare_op=ALU.is_ge, fill=0.0, base=0,
                                       pattern=[[0, HPU], [-1, P]], channel_multiplier=1).then_inc(masked[0], 1)
                else:
                    W = P // 2
                    hi, lo = probs[:, u, :, W:P], probs[:, u, :, 0:W]
                    pool.affine_select(out=hi, in_=hi, compare_op=ALU.is_ge, fill=0.0, base=0,
                                       pattern=[[0, HPU], [-1, W]], channel_multiplier=1)
                    pool.affine_select(out=lo, in_=lo, compare_op=ALU.is_ge, fill=0.0, base=W,
                                       pattern=[[0, HPU], [1, W]], channel_multiplier=-1).then_inc(masked[1], 1)

            def inverse_std(i, k):
                pool.wait_ge(vareps_out[i], k.at(1, 1))
                if due(count := k.at(1, 0)):
                    pool.wait_ge(ln_out[i], count)
                pool.tensor_tensor(rstd[i][:], vareps[i][:], mhalf[:], ALU.pow).then_inc(rstd_out[i], 1)

            def split(name, k, count, ready):
                count = in_register(pool, count)
                pool.wait_ge(const_set, CONSTS)
                pool.wait_ge(ready, count)
                o = k.behind(2)
                if o.exists(NB):
                    count = in_register(pool, o.use_at(16 * TERMS, 16 * TERMS))
                    pool.wait_ge(const_set, CONSTS)
                    pool.wait_ge(stacked[name][o.off // 2 % 2], count)
                pool.tensor_scalar(part[name][:, 1], rest[name][:], 1.0, 0.0, ALU.mult, ALU.add)\
                    .then_inc(part2[name], 1)
                pool.wait_ge(part2[name], k.group_at(1, 1))
                pool.tensor_tensor(part[name][:, 2], rest[name][:], part[name][:, 1], ALU.subtract)\
                    .then_inc(part3[name], 1)

            def slot(s):
                even = s.off % 2 == 0
                t1, t2 = s.behind(T1), s.behind(T2)
                post1, post2, y = (s.behind(n) for n in (POST1, POST2, Y))
                k = s.behind(POST1 + 1)
                if even and k.exists(NB):
                    split("x1", k, k.at(1, 1), rest1["x1"])
                k = s.behind(1)
                if k.exists(NB):
                    split("k" if even else "q", k, k.at(1, 1), qk_rest)
                k = s.behind(4)
                if even and k.exists(NB):
                    split("ctx", k, k.group_at(1, 1), rest1["ctx"])
                k = s.behind(-1)
                if not even and k.exists(NB):
                    ring = k.off // 2 % 2
                    pool.wait_ge(xT_upper, k.group_at(1, 1))
                    pool.tensor_tensor(xT_hl[:, ring, 1], xT_sb[:], xT_hl[:, ring, 0], ALU.subtract)\
                        .then_inc(xT_lower, 1)
                k = s.behind(3)
                if not even and k.exists(NB):
                    ring = k.off // 2 % 2
                    pool.wait_ge(xtok_in[ring], k.use_at(16, 16))
                    for b in range(2):
                        op = pool.tensor_tensor(xtok_sb[:, ring, b], xtok_sb[:, ring, b], bout_sb[:], ALU.add)
                    op.then_inc(xb_ready, 1)
                k = s.behind(4)
                if k.exists(NB):
                    ring = k.off // 2 % 2
                    count = in_register(pool, k.use_at(16, 16))
                    pool.wait_ge(const_set, CONSTS)
                    pool.wait_ge(ctxtok_in[ring], count)
                    if due(count := k.at(UNITS, UNITS * (1 - 4))):
                        count = in_register(pool, count)
                        pool.wait_ge(const_set, CONSTS)
                        pool.wait_ge(pv_done[1], count)
                    pool.tensor_scalar(val2[:, k.off % 4, :, 0:HD],
                                       ctxtok_sb[:, ring, k.off % 2].rearrange("p (h d) -> p h d", h=HEADS),
                                       1.0, 0.0, ALU.mult, ALU.add).then_inc(val2_ready, 1)
                k = s.behind(GATE)
                if k.exists(NB):
                    g, b = k.off // 2 % 2, k.off % 2 * P
                    pool.wait_ge(x2T_upper, k.at(1, 1))
                    pool.tensor_tensor(x2T_hl[:, g, 1, :, b:b + P], x2T[:], x2T_hl[:, g, 0, :, b:b + P],
                                       ALU.subtract).then_inc(x2T_lower, 1)
                for u in range(2):
                    if t2.exists(NB):
                        masking(1, t2, u)
                if post1.exists(NB):
                    inverse_std(0, post1)
                for u in range(2, UNITS):
                    if t2.exists(NB):
                        masking(1, t2, u)
                if y.exists(NB):
                    inverse_std(2, y)
                k = s.behind(POST1 + 1)
                if k.exists(NB):
                    pool.wait_ge(ln_out[0], k.at(1, 1))
                    pool.wait_ge(x1T_psum, k.at(1, 1))
                    pool.tensor_tensor(x1[:, k.off % 4].rearrange("p (t d a) -> p t d a", t=2, d=HD),
                                       x1[:, k.off % 4].rearrange("p (t d a) -> p t d a", t=2, d=HD),
                                       bproj_sb[:].rearrange("p (a t d) -> p t d a", t=2, d=HD), ALU.add)\
                        .then_inc(x1b_ready, 1)
                for u in range(UNITS):
                    if t1.exists(NB):
                        masking(0, t1, u)
                if post2.exists(NB):
                    inverse_std(1, post2)

            run(pool, slot)


def kernel(x, ctx_1024, L0_attn_w_qkv, L0_attn_b_qkv, L0_attn_w_out, L0_attn_b_out, L0_xattn_W_proj,
           L0_xattn_b_proj, L0_ffn_gate_w, L0_ffn_Wu, L0_ffn_Wv, L0_ffn_Wo):
    import ml_dtypes
    import numpy as np
    import concourse.bacc as bacc
    from concourse.bass_utils import run_bass_kernel_spmd

    x, c, wqkv, bqkv, wout, bout, wproj, bproj, gw, wu, wv, wo = (
        np.asarray(a) for a in (x, ctx_1024, L0_attn_w_qkv, L0_attn_b_qkv, L0_attn_w_out, L0_attn_b_out,
                                L0_xattn_W_proj, L0_xattn_b_proj, L0_ffn_gate_w, L0_ffn_Wu, L0_ffn_Wv, L0_ffn_Wo))
    NB, S = x.shape[:2]
    NG = NB // 2
    bf16 = ml_dtypes.bfloat16
    qk_w = wqkv[:, :2 * D].reshape(D, 2, 8, 2, HD).transpose(0, 1, 3, 4, 2).reshape(D, 2 * D)
    i, j = np.arange(P)[:, None], np.arange(P)[None, :]
    allowed = np.stack([j >= i, abs(i - j) <= 64], axis=1)
    rows3 = np.arange(3 * E)
    arrays = dict(
        x=x,
        xT=x.reshape(NG, 2, S, KT, P).transpose(0, 4, 3, 1, 2).reshape(NG, P, KT, 2 * S),
        ctx_tok=c,
        ctxT=c.reshape(NG, 2, S, 8, 2, HD).transpose(0, 5, 3, 4, 1, 2).reshape(NG, P, 2, 2 * S),
        w_qkv=np.concatenate([qk_w, wqkv[:, 2 * D:]], axis=1),
        b_qk=bqkv[:2 * D].reshape(2, 8, 2, HD).transpose(3, 1, 0, 2).reshape(P, 4),
        b_v=bqkv[2 * D:].reshape(KT, P).T, w_out=wout, b_out=bout, w_proj=wproj.T, b_proj=bproj, gate_w=gw,
        w_u=wu.transpose(1, 0, 2).reshape(D, E * R), w_v=wv.transpose(1, 0, 2).reshape(D, E * R),
        w_o=wo.reshape(E * R, D),
        ident=np.eye(P, dtype=np.float32),
        ident_bf=np.eye(P).astype(bf16),
        masks=np.where(allowed, 0.0, -3e38).astype(bf16),
        expert_sel=(rows3[:, None, None] % E == 2 * np.arange(FT)[:, None] + np.arange(P) // R).astype(bf16),
        iota8=np.arange(E, dtype=np.float32),
    )
    arrays = {n: np.ascontiguousarray(a) for n, a in arrays.items()}
    nc = bacc.Bacc("TRN2", target_bir_lowering=False, num_devices=1)
    args = {n: nc.dram_tensor(f"in_{n}", a.shape, mybir.dt.from_np(a.dtype), kind="ExternalInput").ap()
            for n, a in arrays.items()}
    out = nc.dram_tensor("out", x.shape, F32, kind="ExternalOutput").ap()
    decoder_layer(nc, **args, out=out)
    r = run_bass_kernel_spmd(nc, [{f"in_{n}": a for n, a in arrays.items()}], core_ids=[0])
    return r.results[0]["out"]
```
